# Optimizing a Trainium2 kernel written in Bass

```python
import numpy as np
import jax
import jax.numpy as jnp

def _softmax(x, axis=-1):
    return jax.nn.softmax(x, axis=axis)

def _gelu(x):
    return jax.nn.gelu(x, approximate=True)

def _silu(x):
    return jax.nn.silu(x)

def _sigmoid(x):
    return jax.nn.sigmoid(x)

def _layernorm(x, axis=-1, eps=1e-05):
    m = jnp.mean(x, axis=axis, keepdims=True)
    v = jnp.var(x, axis=axis, keepdims=True)
    return (x - m) / jnp.sqrt(v + eps)

def _scatter_add(tgt, idx, src, axis=0):
    return tgt.at[idx].add(src)

def _segment_sum(src, seg, n):
    return jax.ops.segment_sum(src, seg, n)
kernel_name = 'mk_decoder_preln_d1_seqx_r4_00ddbd'

def setup_inputs(seed: int=0):
    np.random.seed(seed)
    _w = jnp.asarray

    def _rec_inputs():
        import jax
        import jax.numpy as jnp
        _rk = jax.random.key(seed)
        x = -0.0003929 + 0.9999 * jax.random.normal(jax.random.fold_in(_rk, 1), (8, 256, 512), jnp.float32)
        _lenS = 256 - jax.random.randint(jax.random.fold_in(_rk, 7), (8,), 0, max(1, 256 // 4) + 1, jnp.int32)
        _lenS2 = 256 - jax.random.randint(jax.random.fold_in(_rk, 8), (8,), 0, max(1, 256 // 4) + 1, jnp.int32)
        _ctx_2048P = jax.random.normal(jax.random.fold_in(_rk, 11), (8, 16, 512), jnp.float32)
        _ctx_2048c = jax.random.dirichlet(jax.random.fold_in(_rk, 511), 0.3 * jnp.ones((16,), jnp.float32), (8, 256))
        _ctx_2048t = jnp.einsum('bsk,bkd->bsd', _ctx_2048c, _ctx_2048P)
        _ctx_2048t = _ctx_2048t * jax.lax.rsqrt(jnp.mean(jnp.square(_ctx_2048t)) + 1e-12) * 0.953939
        ctx_2048 = -1.39393e-06 + 0.999914 * (_ctx_2048t + 0.3 * jax.random.normal(jax.random.fold_in(_rk, 611), (8, 256, 512), jnp.float32))
        itok_BxS_0_1023 = jax.random.randint(jax.random.fold_in(_rk, 12), (8, 256), 0, 256, jnp.int32)
        return (x, ctx_2048, itok_BxS_0_1023)
    x, ctx_2048, itok_BxS_0_1023 = _rec_inputs()

    def _L0_attn_setup():
        import jax, jax.numpy as jnp
        import numpy as np
        C = 512
        A = 512
        HS = 64
        H = A // HS
        DMIX = 32
        DDEC = 64
        B, T = (2, 512)
        EPS = 1e-05 * 8.0 ** 2
        key = jax.random.key(seed)
        ks = jax.random.split(key, 20)
        n = lambda i, shape, s=0.02: jax.random.normal(ks[i], shape, dtype=jnp.float32) * s
        return dict(hidden=jax.random.normal(ks[0], (B, T, C), dtype=jnp.float32), time_maa_x=n(1, (1, 1, C), 0.5), time_maa_w=n(2, (1, 1, C), 0.5), time_maa_k=n(3, (1, 1, C), 0.5), time_maa_v=n(4, (1, 1, C), 0.5), time_maa_r=n(5, (1, 1, C), 0.5), time_maa_g=n(6, (1, 1, C), 0.5), time_maa_w1=n(7, (C, DMIX * 5)), time_maa_w2=n(8, (5, DMIX, C)), time_decay=n(9, (1, 1, A), 0.5), time_decay_w1=n(10, (C, DDEC)), time_decay_w2=n(11, (DDEC, A)), time_faaaa=n(12, (H, HS), 0.5), W_r=n(13, (A, C)), W_k=n(14, (A, C)), W_v=n(15, (A, C)), W_g=n(16, (A, C)), W_o=n(17, (C, A)), ln_gamma=jnp.ones((C,), jnp.float32), ln_beta=jnp.zeros((C,), jnp.float32))
    _L0_attn_all = _L0_attn_setup()
    _L0_attn_in = {k: v for k, v in _L0_attn_all.items() if k in ('time_maa_x', 'time_maa_w', 'time_maa_k', 'time_maa_v', 'time_maa_r', 'time_maa_g', 'time_maa_w1', 'time_maa_w2', 'time_decay', 'time_decay_w1', 'time_decay_w2', 'time_faaaa', 'W_r', 'W_k', 'W_v', 'W_g', 'W_o', 'ln_gamma', 'ln_beta')}
    del _L0_attn_all

    def _L0_xattn_setup():
        import jax, jax.numpy as jnp
        import numpy as np
        B, Lq, Lk = (2, 1024, 256)
        Q_DIM, KV_DIM = (512, 512)
        H, HD = (16, 128)
        KVC, QC, R = (128, 192, 64)
        LOOKBACK = 8
        NEG = -1e+30

        def _rope(x, L):
            half = x.shape[-1] // 2
            inv_freq = 1.0 / 10000.0 ** (jnp.arange(half, dtype=jnp.float32) / half)
            ang = jnp.arange(L, dtype=jnp.float32)[:, None] * inv_freq
            cos, sin = (jnp.cos(ang), jnp.sin(ang))
            x1, x2 = (x[..., :half], x[..., half:])
            return jnp.concatenate([x1 * cos - x2 * sin, x1 * sin + x2 * cos], axis=-1)
        key = jax.random.key(seed)
        ks = jax.random.split(key, 11)

        def w(k, shape, fan_in):
            return jax.random.normal(k, shape, jnp.float32) / np.sqrt(fan_in).astype(np.float32)
        return {'q': jax.random.normal(ks[0], (B, Lq, Q_DIM), jnp.float32), 'kv': jax.random.normal(ks[1], (B, Lk, KV_DIM), jnp.float32), 'seg_id': jnp.sort(jax.random.randint(ks[2], (B, Lq), 0, Lk), axis=-1), 'W_kvc': w(ks[3], (KV_DIM, KVC), KV_DIM), 'W_dq': w(ks[4], (Q_DIM, QC), Q_DIM), 'W_uq': w(ks[5], (QC, H * HD), QC), 'W_qr': w(ks[6], (QC, H * R), QC), 'W_uk': w(ks[7], (KVC, H * HD), KVC), 'W_kr': w(ks[8], (KVC, R), KVC), 'W_uv': w(ks[9], (KVC, H * HD), KVC), 'W_o': w(ks[10], (H * HD, Q_DIM), H * HD)}
    _L0_xattn_all = _L0_xattn_setup()
    _L0_xattn_in = {k: v for k, v in _L0_xattn_all.items() if k in ('W_kvc', 'W_dq', 'W_uq', 'W_qr', 'W_uk', 'W_kr', 'W_uv', 'W_o')}
    del _L0_xattn_all

    def _L0_ffn_setup():
        import jax, jax.numpy as jnp
        import numpy as np
        H = 512
        I = 352
        E = 8
        K = 2
        B, S = (4, 512)

        def _moe(x, router_w, w1, w2):
            b, s, h = x.shape
            xf = x.reshape(-1, h)
            T = xf.shape[0]
            logits = xf @ router_w.T
            topk_vals, topk_idx = jax.lax.top_k(logits, K)
            topk_w = jax.nn.softmax(topk_vals, axis=-1)
            exp_id = topk_idx.reshape(-1)
            exp_w = topk_w.reshape(-1)
            order = jnp.argsort(exp_id)
            x_sorted = xf[order // K]
            counts = jnp.bincount(exp_id, length=E).astype(jnp.int32)
            y1 = jax.lax.ragged_dot(x_sorted, jnp.swapaxes(w1, 1, 2), counts)
            gate, up = jnp.split(y1, 2, axis=-1)
            y_act = jax.nn.silu(gate) * up
            y2 = jax.lax.ragged_dot(y_act, jnp.swapaxes(w2, 1, 2), counts)
            inv = jnp.argsort(order)
            y_pairs = y2[inv] * exp_w[:, None]
            y = y_pairs.reshape(T, K, h).sum(axis=1)
            return y.reshape(b, s, h)
        key = jax.random.key(seed)
        k1, k2, k3, k4 = jax.random.split(key, 4)
        x = jax.random.normal(k1, (B, S, H), dtype=jnp.float32)
        router_w = jax.random.normal(k2, (E, H), dtype=jnp.float32) * 0.02
        w1 = jax.random.normal(k3, (E, 2 * I, H), dtype=jnp.float32) * 0.02
        w2 = jax.random.normal(k4, (E, H, I), dtype=jnp.float32) * 0.02
        return {'x': x, 'router_w': router_w, 'w1': w1, 'w2': w2}
    _L0_ffn_all = _L0_ffn_setup()
    _L0_ffn_in = {k: v for k, v in _L0_ffn_all.items() if k in ('router_w', 'w1', 'w2')}
    del _L0_ffn_all
    return {'x': x, 'ctx_2048': ctx_2048, 'itok_BxS_0_1023': itok_BxS_0_1023, 'L0_attn_time_maa_x': _L0_attn_in['time_maa_x'], 'L0_attn_time_maa_w': _L0_attn_in['time_maa_w'], 'L0_attn_time_maa_k': _L0_attn_in['time_maa_k'], 'L0_attn_time_maa_v': _L0_attn_in['time_maa_v'], 'L0_attn_time_maa_r': _L0_attn_in['time_maa_r'], 'L0_attn_time_maa_g': _L0_attn_in['time_maa_g'], 'L0_attn_time_maa_w1': _L0_attn_in['time_maa_w1'], 'L0_attn_time_maa_w2': _L0_attn_in['time_maa_w2'], 'L0_attn_time_decay': _L0_attn_in['time_decay'], 'L0_attn_time_decay_w1': _L0_attn_in['time_decay_w1'], 'L0_attn_time_decay_w2': _L0_attn_in['time_decay_w2'], 'L0_attn_time_faaaa': _L0_attn_in['time_faaaa'], 'L0_attn_W_r': _L0_attn_in['W_r'], 'L0_attn_W_k': _L0_attn_in['W_k'], 'L0_attn_W_v': _L0_attn_in['W_v'], 'L0_attn_W_g': _L0_attn_in['W_g'], 'L0_attn_W_o': _L0_attn_in['W_o'], 'L0_attn_ln_gamma': _L0_attn_in['ln_gamma'], 'L0_attn_ln_beta': _L0_attn_in['ln_beta'], 'L0_xattn_W_kvc': _L0_xattn_in['W_kvc'], 'L0_xattn_W_dq': _L0_xattn_in['W_dq'], 'L0_xattn_W_uq': _L0_xattn_in['W_uq'], 'L0_xattn_W_qr': _L0_xattn_in['W_qr'], 'L0_xattn_W_uk': _L0_xattn_in['W_uk'], 'L0_xattn_W_kr': _L0_xattn_in['W_kr'], 'L0_xattn_W_uv': _L0_xattn_in['W_uv'], 'L0_xattn_W_o': _L0_xattn_in['W_o'], 'L0_ffn_router_w': _L0_ffn_in['router_w'], 'L0_ffn_w1': _L0_ffn_in['w1'], 'L0_ffn_w2': _L0_ffn_in['w2']}

def reference(x, ctx_2048, itok_BxS_0_1023, L0_attn_time_maa_x, L0_attn_time_maa_w, L0_attn_time_maa_k, L0_attn_time_maa_v, L0_attn_time_maa_r, L0_attn_time_maa_g, L0_attn_time_maa_w1, L0_attn_time_maa_w2, L0_attn_time_decay, L0_attn_time_decay_w1, L0_attn_time_decay_w2, L0_attn_time_faaaa, L0_attn_W_r, L0_attn_W_k, L0_attn_W_v, L0_attn_W_g, L0_attn_W_o, L0_attn_ln_gamma, L0_attn_ln_beta, L0_xattn_W_kvc, L0_xattn_W_dq, L0_xattn_W_uq, L0_xattn_W_qr, L0_xattn_W_uk, L0_xattn_W_kr, L0_xattn_W_uv, L0_xattn_W_o, L0_ffn_router_w, L0_ffn_w1, L0_ffn_w2):
    import jax
    import jax.numpy as jnp

    def _L0_attn_ref(hidden, time_maa_x, time_maa_w, time_maa_k, time_maa_v, time_maa_r, time_maa_g, time_maa_w1, time_maa_w2, time_decay, time_decay_w1, time_decay_w2, time_faaaa, W_r, W_k, W_v, W_g, W_o, ln_gamma, ln_beta):
        import jax, jax.numpy as jnp
        import numpy as np
        C = 512
        A = 512
        HS = 64
        H = A // HS
        DMIX = 32
        DDEC = 64
        B, T = (2, 512)
        EPS = 1e-05 * 8.0 ** 2
        Bq, Tq, Cq = hidden.shape
        shifted = jnp.pad(hidden, ((0, 0), (1, 0), (0, 0)))[:, :-1]
        xx = shifted - hidden
        xxx = hidden + xx * time_maa_x
        z = jnp.tanh(jnp.einsum('btc,cd->btd', xxx, time_maa_w1)).reshape(Bq, Tq, 5, DMIX)
        mix = jnp.einsum('btfd,fdc->fbtc', z, time_maa_w2)
        mw, mk, mv, mr, mg = (mix[0], mix[1], mix[2], mix[3], mix[4])
        xw = hidden + xx * (time_maa_w + mw)
        xk = hidden + xx * (time_maa_k + mk)
        xv = hidden + xx * (time_maa_v + mv)
        xr = hidden + xx * (time_maa_r + mr)
        xg = hidden + xx * (time_maa_g + mg)
        r = jnp.einsum('btc,ac->bta', xr, W_r)
        k = jnp.einsum('btc,ac->bta', xk, W_k)
        v = jnp.einsum('btc,ac->bta', xv, W_v)
        g = jax.nn.silu(jnp.einsum('btc,ac->bta', xg, W_g))
        dd = jnp.einsum('btd,da->bta', jnp.tanh(jnp.einsum('btc,cd->btd', xw, time_decay_w1)), time_decay_w2) + time_decay
        w = jnp.exp(-jnp.exp(dd))
        rh = r.reshape(Bq, Tq, H, HS).transpose(1, 0, 2, 3)
        kh = k.reshape(Bq, Tq, H, HS).transpose(1, 0, 2, 3)
        vh = v.reshape(Bq, Tq, H, HS).transpose(1, 0, 2, 3)
        wh = w.reshape(Bq, Tq, H, HS).transpose(1, 0, 2, 3)
        u = time_faaaa

        def step(S, inputs):
            r_t, k_t, v_t, w_t = inputs
            kv = k_t[..., :, None] * v_t[..., None, :]
            out_t = jnp.einsum('bhn,bhnm->bhm', r_t, u[None, :, :, None] * kv + S)
            S = kv + w_t[..., :, None] * S
            return (S, out_t)
        S0 = jnp.zeros((Bq, H, HS, HS), dtype=hidden.dtype)
        _, outs = jax.lax.scan(step, S0, (rh, kh, vh, wh))
        out = outs.transpose(1, 0, 2, 3)
        mean = out.mean(-1, keepdims=True)
        var = out.var(-1, keepdims=True)
        out = (out - mean) * jax.lax.rsqrt(var + EPS)
        out = out.reshape(Bq, Tq, Cq) * ln_gamma + ln_beta
        out = out * g
        return jnp.einsum('bta,ca->btc', out, W_o)

    def _L0_xattn_ref(q, kv, seg_id, W_kvc, W_dq, W_uq, W_qr, W_uk, W_kr, W_uv, W_o):
        import jax, jax.numpy as jnp
        import numpy as np
        B, Lq, Lk = (2, 1024, 256)
        Q_DIM, KV_DIM = (512, 512)
        H, HD = (16, 128)
        KVC, QC, R = (128, 192, 64)
        LOOKBACK = 8
        NEG = -1e+30

        def _rope(x, L):
            half = x.shape[-1] // 2
            inv_freq = 1.0 / 10000.0 ** (jnp.arange(half, dtype=jnp.float32) / half)
            ang = jnp.arange(L, dtype=jnp.float32)[:, None] * inv_freq
            cos, sin = (jnp.cos(ang), jnp.sin(ang))
            x1, x2 = (x[..., :half], x[..., half:])
            return jnp.concatenate([x1 * cos - x2 * sin, x1 * sin + x2 * cos], axis=-1)
        b, lq, _ = q.shape
        lk = kv.shape[1]
        kv_c = kv @ W_kvc
        q_c = q @ W_dq
        q_nope = (q_c @ W_uq).reshape(b, lq, H, HD).transpose(0, 2, 1, 3)
        q_rope = (q_c @ W_qr).reshape(b, lq, H, R).transpose(0, 2, 1, 3)
        k_nope = (kv_c @ W_uk).reshape(b, lk, H, HD)
        v = (kv_c @ W_uv).reshape(b, lk, H, HD)
        k_rope = kv_c @ W_kr
        q_rope = _rope(q_rope, lq)
        k_rope = _rope(k_rope, lk)
        scale = 1.0 / np.sqrt(HD + R).astype(np.float32)
        scores = (jnp.einsum('bhqd,bkhd->bhqk', q_nope, k_nope) + jnp.einsum('bhqr,bkr->bhqk', q_rope, k_rope)) * scale
        k_ids = jnp.arange(lk)[None, None, :]
        qs = seg_id[:, :, None]
        good = (k_ids <= qs) & (k_ids >= qs - LOOKBACK)
        scores = jnp.where(good[:, None, :, :], scores, NEG)
        attn = jax.nn.softmax(scores, axis=-1)
        out = jnp.einsum('bhqk,bkhd->bqhd', attn, v).reshape(b, lq, H * HD)
        return out @ W_o

    def _L0_ffn_ref(x, router_w, w1, w2):
        import jax, jax.numpy as jnp
        import numpy as np
        H = 512
        I = 352
        E = 8
        K = 2
        B, S = (4, 512)

        def _moe(x, router_w, w1, w2):
            b, s, h = x.shape
            xf = x.reshape(-1, h)
            T = xf.shape[0]
            logits = xf @ router_w.T
            topk_vals, topk_idx = jax.lax.top_k(logits, K)
            topk_w = jax.nn.softmax(topk_vals, axis=-1)
            exp_id = topk_idx.reshape(-1)
            exp_w = topk_w.reshape(-1)
            order = jnp.argsort(exp_id)
            x_sorted = xf[order // K]
            counts = jnp.bincount(exp_id, length=E).astype(jnp.int32)
            y1 = jax.lax.ragged_dot(x_sorted, jnp.swapaxes(w1, 1, 2), counts)
            gate, up = jnp.split(y1, 2, axis=-1)
            y_act = jax.nn.silu(gate) * up
            y2 = jax.lax.ragged_dot(y_act, jnp.swapaxes(w2, 1, 2), counts)
            inv = jnp.argsort(order)
            y_pairs = y2[inv] * exp_w[:, None]
            y = y_pairs.reshape(T, K, h).sum(axis=1)
            return y.reshape(b, s, h)
        return _moe(x, router_w, w1, w2)
    x = x + _L0_attn_ref(_layernorm(x, axis=-1), L0_attn_time_maa_x, L0_attn_time_maa_w, L0_attn_time_maa_k, L0_attn_time_maa_v, L0_attn_time_maa_r, L0_attn_time_maa_g, L0_attn_time_maa_w1, L0_attn_time_maa_w2, L0_attn_time_decay, L0_attn_time_decay_w1, L0_attn_time_decay_w2, L0_attn_time_faaaa, L0_attn_W_r, L0_attn_W_k, L0_attn_W_v, L0_attn_W_g, L0_attn_W_o, L0_attn_ln_gamma, L0_attn_ln_beta)
    x = x + _L0_xattn_ref(_layernorm(x, axis=-1), ctx_2048, itok_BxS_0_1023, L0_xattn_W_kvc, L0_xattn_W_dq, L0_xattn_W_uq, L0_xattn_W_qr, L0_xattn_W_uk, L0_xattn_W_kr, L0_xattn_W_uv, L0_xattn_W_o)
    x = x + _L0_ffn_ref(_layernorm(x, axis=-1), L0_ffn_router_w, L0_ffn_w1, L0_ffn_w2)
    return x

_drawn_inputs = setup_inputs


def setup_inputs(seed=0):
    import zlib

    import numpy as np

    out = dict(_drawn_inputs(seed))
    spreads = {'L0_attn_ln_gamma': (1.0, 0.6), 'L0_attn_ln_beta': (0.0, 0.658)}
    factors = {'L0_attn_time_maa_x': 5.231,
     'L0_attn_time_maa_w': 8.0,
     'L0_attn_time_maa_w1': 3.135,
     'L0_attn_time_maa_w2': 3.132,
     'L0_attn_time_decay_w1': 8.0,
     'L0_attn_time_decay_w2': 8.0,
     'L0_ffn_router_w': 2.675}
    for name, (base, spread) in spreads.items():
        noise = np.random.default_rng([zlib.crc32(name.encode()), seed]).standard_normal(out[name].shape)
        drawn = base * np.exp(spread * noise) if base else spread * noise
        out[name] = jnp.asarray(drawn.astype(out[name].dtype))
    for name, factor in factors.items():
        out[name] = (out[name] * factor).astype(out[name].dtype)
    return out
```

```python
from contextlib import ExitStack

import numpy as np
import concourse.bass as bass
from concourse import mybir

F32 = mybir.dt.float32
BF16 = mybir.dt.bfloat16
I32 = mybir.dt.int32
U8 = mybir.dt.uint8
U32 = mybir.dt.uint32
ALU = mybir.AluOpType
ACT = mybir.ActivationFunctionType
AX = mybir.AxisListType

P = 128
B, T, C = 8, 256, 512
KT = C // P
HALF = T // P
RH, HS = 8, 64
MIX, DMIX, DDEC = 5, 32, 64
LN_EPS, GN_EPS = 1e-5, 1e-5 * 8.0 ** 2
LEVELS = 8
XH, HD, ROT = 16, 128, 64
KVC, QC = 128, 192
QK = QC // 2
LOOKBACK, NEG = 8, -1e30
SCALE = 1.0 / np.sqrt(HD + ROT)
E, I, TOP = 8, 352, 8
CHOICES = 2
IT = 3
INNER = [(0, 128), (128, 128), (256, 96)]
NT = B * T // P
REGION = B * T + P
SPARE = E * REGION
STEPS = (CHOICES * B * T // P + E - 1 + 1) // 2 * 2
DECAY_CAP = 60.0


def constants():
    s, t = np.arange(P)[:, None], np.arange(P)[None, :]
    gap = np.zeros((P, HALF, LEVELS - 1, P), np.float32)
    for level in range(1, LEVELS - 1):
        h = 1 << level
        middle = (t // (2 * h)) * 2 * h + h
        between = np.where(t < middle, (s > t) & (s < middle), (s >= middle) & (s < t))
        gap[:, :, level, :] = -between.astype(np.float32)[:, None, :]
    gap[:, 0, 0, :] = -1.0 * (s > t)
    gap[:, 1, 0, :] = -1.0 * (s < t)
    pick = np.zeros((P, 6, HALF, P), np.int32)
    pick[:, 0] = (s == t)[:, None, :]
    for level in range(5):
        h = 1 << level
        same = (s // (2 * h) == t // (2 * h)) & (s % (2 * h) < h) & (t % (2 * h) >= h)
        pick[:, level + 1] = same[:, None, :]
    half = ROT // 2
    inv = (1.0 / 10000.0 ** (np.arange(half, dtype=np.float32) / half)).astype(np.float32)
    ang = (np.arange(T, dtype=np.float32)[:, None] * inv).astype(np.float32)
    cos, sin = np.cos(ang).T.astype(np.float32), np.sin(ang).T.astype(np.float32)
    q_rot = np.concatenate([cos, cos, sin, sin])
    q_table = np.stack([np.ones((P, T), np.float32), q_rot], 1) * np.float32(SCALE)
    q_table = q_table.reshape(P, 2, HALF, P).transpose(0, 2, 1, 3)
    k_table = np.stack([np.concatenate([cos, cos, cos, -cos]), np.concatenate([-sin, sin, sin, sin])], 1)
    before = np.concatenate([(s < t).astype(np.float32), np.ones((P, P), np.float32)], 1)
    return {
        "c_before": before,
        "c_gap": gap.reshape(P, -1),
        "c_pick": pick.reshape(P, -1),
        "c_ident": np.eye(P, dtype=np.float32),
        "c_keys": np.tile(np.arange(T, dtype=np.float32), (P, 1)),
        "c_qtab": np.ascontiguousarray(q_table.reshape(P, -1)),
        "c_ktab": np.ascontiguousarray(k_table.reshape(P, -1)),
    }


class Arena:

    def __init__(self, tensor, words):
        self.tensor, self.words, self.at = tensor, words, 0

    def take(self, n):
        a = self.tensor[:, self.at:self.at + n]
        self.at += n
        assert self.at <= self.words, self.at
        return a


def program(nc, d, out, x2_dram, xs, ys):
    with ExitStack() as ctx:
        WORDS = 52264
        space = ctx.enter_context(nc.sbuf_tensor("space", [P, WORDS], F32))
        ps = ctx.enter_context(nc.psum_tensor("ps", [P, 8, 512], F32))
        ident_bf = ctx.enter_context(nc.sbuf_tensor("ident_bf", [P, P], BF16))

        minus_half = ctx.enter_context(nc.sbuf_tensor("minus_half", [P, 4], F32))

        def sem(name):
            return ctx.enter_context(nc.semaphore(name))

        ar = Arena(space, WORDS)

        def tiles(n, k):
            return ar.take(n).rearrange("p (k n) -> p k n", k=k)

        gap = tiles(HALF * 7 * P, HALF)
        pick = ar.take(6 * HALF * P // 4).bitcast(U8).rearrange("p (l n) -> p l n", l=6)
        ident = ar.take(P)
        keys = ar.take(T)
        qtab = tiles(HALF * 2 * P, HALF)
        ktab = tiles(2 * T, 2)
        w1 = tiles(KT * MIX * DMIX, KT)
        w2 = tiles(2 * C, 2)
        maa = tiles((MIX + 1) * KT, MIX + 1)
        dw1 = tiles(KT * DDEC, KT)
        dw2 = ar.take(C)
        bonus = ar.take(KT)
        gam = ar.take(KT)
        bet = ar.take(KT)
        wr, wk, wv, wg, wo = (tiles(KT * C, KT) for _ in range(5))
        wkvc = tiles(KT * KVC, KT)
        wkr = tiles(2 * P, 2)
        wdq = tiles(KT * QC, KT)
        wqr = tiles(2 * XH * 2 * ROT, 2)
        wqk = tiles(2 * XH * KVC, 2)
        wvo = tiles(XH * C, XH)
        ar.take(ar.at % 2)
        start_of_work = ar.at
        x_in, x1, xn = (tiles(HALF * C, HALF) for _ in range(3))
        half_gate = xn
        o_tok = xn
        hT = tiles(KT * (T + 1), KT)
        xx, gT, oT = (tiles(KT * T, KT) for _ in range(3))
        xxx = gT
        e_tok = oT.rearrange("p k n -> p (k n)").rearrange("p (k n) -> p k n", k=HALF)
        rT, kT = (tiles(KT * T, KT) for _ in range(2))
        v_tok = tiles(HALF * C, HALF)
        z_a, z_b, z_dec = (ar.take(T) for _ in range(3))
        q_at = ar.at
        lev = [tiles(7 * T, 7) for _ in range(2)]
        mixed_x = [q.rearrange("p l n -> p (l n)")[:, 0:KT * T].rearrange("p (k n) -> p k n", k=KT) for q in lev]
        ru = [ar.take(T) for _ in range(2)]
        a_near = [tiles(HALF * P, HALF) for _ in range(2)]
        a_far = [ar.take(P) for _ in range(2)]
        ctx_at = ar.at
        ctxT = tiles(KT * T, KT)
        kvcT, krT, kr_tmp = (ar.take(T) for _ in range(3))
        kvc = tiles(HALF * KVC, HALF)
        st1, mv1, rstd1 = tiles(HALF * 6, HALF), tiles(HALF * 2, HALF), ar.take(HALF)
        st23, mv23, rstd23 = tiles(HALF * 6, HALF), tiles(HALF * 2, HALF), ar.take(HALF)
        gst, gmv, grstd = tiles(2 * 24, 2), tiles(2 * 8, 2), tiles(2 * 4, 2)
        segi = ar.take(HALF)
        segf, negmax, psumr, prec = ar.take(HALF), ar.take(4), ar.take(4), ar.take(4)
        aq = Arena(space, WORDS)
        aq.at = q_at
        q_lat = aq.take(2 * T).rearrange("p (k n) -> p k n", k=2)
        bias = aq.take(HALF * T // 2).bitcast(BF16).rearrange("p (k n) -> p k n", k=HALF)
        late, early = aq.take(T), aq.take(T)
        q_head = [aq.take(2 * P).rearrange("p (k n) -> p k n", k=2) for _ in range(2)]
        prob = [aq.take(T) for _ in range(3)]
        probT = [aq.take(T).rearrange("p (k n) -> p k n", k=2) for _ in range(2)]
        o_head = [aq.take(P) for _ in range(2)]
        assert aq.at <= q_at + 2 * 7 * T
        x1T = xx
        ap = Arena(space, WORDS)
        ap.at = start_of_work
        uqT = ap.take(XH * QC).rearrange("p (h n) -> p h n", h=XH)
        ukT = ap.take(XH * KVC).rearrange("p (h n) -> p h n", h=XH)
        uvT = ap.take(XH * KVC).rearrange("p (h n) -> p h n", h=XH)
        xo = ap.take(XH * C).rearrange("p (h n) -> p h n", h=XH)

        ap.at = ctx_at
        pick_wide = ap.take(6 * HALF * P).bitcast(I32)

        def small(name, *shape, dt=F32):
            return ctx.enter_context(nc.sbuf_tensor(name, [P, *shape], dt))

        before = small("before", 2, P)
        router = small("router", KT, E)
        iota_e = small("iota_e", E)
        logit = small("logit", HALF, E)
        top, topi, topf = small("top", HALF, TOP), small("topi", HALF, TOP, dt=U32), small("topf", HALF, TOP)
        odds = small("odds", 4, HALF)
        hot = small("hot", HALF, CHOICES, E)
        both = small("both", HALF, E)
        place = small("place", HALF, E)
        picked = small("picked", HALF, CHOICES, E)
        slotf = small("slotf", HALF * CHOICES)
        slot = small("slot", HALF * CHOICES, dt=I32)
        taken = small("taken", E)
        slots = small("slots", NT * CHOICES)
        rows = small("rows", NT * CHOICES, dt=I32)
        experts_of = small("experts_of", NT * CHOICES)
        weights = small("weights", NT * CHOICES)
        n_tiles, n_int, ends = small("n_tiles", E), small("n_int", E, dt=I32), small("ends", 2, E)
        count_int = small("count_int", E, dt=I32)
        steps = small("steps", STEPS + 2)
        step_tab = small("step_tab", 2, STEPS + 2, dt=I32)
        first_row = small("first_row", E)
        x3, x3T = v_tok, rT

        am = Arena(space, WORDS)
        am.at = HALF * 7 * P + 6 * HALF * P // 4
        assert am.take(P).shape == ident.shape
        w_gu = am.take(E * 2 * KT * I)
        w_dn = am.take(E * IT * C)
        zeros = am.take(C)
        chosen = am.take(NT * CHOICES * E).rearrange("p (n e) -> p n e", e=E)
        moved = am.take(NT * CHOICES)
        is_past, past_tiles, step_e, step_row = (am.take(STEPS + 2) for _ in range(4))
        m_x = [am.take(C) for _ in range(2)]
        m_xT = [am.take(C).rearrange("p (k n) -> p k n", k=KT) for _ in range(2)]
        m_tanh, m_silu, m_h = (am.take(I) for _ in range(3))
        m_hT = [am.take(IT * P).rearrange("p (k n) -> p k n", k=IT) for _ in range(2)]
        m_y = [am.take(C) for _ in range(2)]
        res = [am.take(C) for _ in range(3)]
        y_of = [[am.take(C) for _ in range(CHOICES)] for _ in range(3)]

        s = {n: sem(n) for n in (
            "consts_in", "front_in", "proj_in", "absorb_in", "cross_in", "ones_set", "ident_bf_set",
            "absorb_mm", "absorb_done", "x_in_loaded", "ctx_in", "seg_in",
            "ln1_raw", "ln1_stats", "ln1_rstd", "ln1_normed", "h_transposed", "h_ready", "xx_ready", "xxx_ready",
            "z_mm", "z_ready", "mix_mm", "mix_used", "mixed_ready", "zdec_mm", "zdec_ready", "k_mm", "k_ready",
            "dd_mm", "dd_capped", "e_ready", "v_mm", "v_ready", "r_mm", "r_ready", "g_mm", "g_tanh", "g_ready",
            "gap_mm", "decays_ready", "k_decayed", "r_decayed", "gram_far", "gram_near", "far_copied", "near_picked",
            "av_done", "gn_raw", "gn_stats", "gn_rstd", "o_normed", "o_transposed", "o_affine", "o_gated",
            "wo_mm", "x1_ready",
            "kvc_mm", "kvc_ready", "kr_mm", "kr_cos", "kr_sin", "kr_ready",
            "seg_float", "late_set", "early_set", "bad_set", "bias_ready",
            "ln2_raw", "ln2_stats", "ln2_rstd", "ln2_normed", "x1_transposed", "x1T_ready", "qlat_mm", "qlat_ready",
            "head_mm", "head_ready", "score_mm", "max_ready", "exp_done", "sum_inverted", "prob_ready",
            "prob_transposed", "probT_ready", "pv_mm", "o_head_ready", "out_mm", "x2_ready", "x2_stored",
            "router_in", "route_link", "ln3_raw", "ln3_stats", "ln3_rstd", "ln3_normed", "x3_transposed", "x3T_ready",
            "logit_mm", "topi_ready", "gap12", "odds_ready", 
            "w_kept", "both_ready", "rank_mm", "taken_moved", 
            "slot_ready", "slots_kept", "scattered", "table_link", "table_ready", "padded",
            "expert_ready", "gate_mm", "up_mm", "m_x_in_0", "m_x_in_1", "m_x_transposed", "m_xT_ready", "m_tanhed", "m_silued",
            "m_h_ready", "m_h_transposed", "m_hT_ready", "down_mm", "m_y_ready", "m_y_stored_0", "m_y_stored_1",
            "res_in_0", "res_in_1", "res_in_2", "y_in_0", "y_in_1", "y_in_2", "first_added", "summed", "stored_0", "stored_1", "stored_2",
            "waited_apart",
            "ln1_rstd_sum", "ln2_rstd_sum", "ln3_rstd_sum", "gn_rstd_sum", "level_picked",
        )}
        expert_in = [sem(f"expert_in_{n}") for n in range(E)]

        def after(eng, signal, n):
            if not isinstance(n, int) or n > 0:
                eng.wait_ge(s[signal], n)

        def wait_apart(eng, signal, n):
            eng.wait_ge(s[signal], n)
            eng.sem_inc(s["waited_apart"], 1)

        block = ctx.enter_context(nc.Block())

        def bank(n, *shape):
            return ps[:, n, :]

        def tok(a):
            return a

        gap_words = HALF * 7 * P

        @block.sync
        def _(sp):
            def load(dst, name, signal):
                sp.dma_start(dst, d[name]).then_inc(s[signal], 16)

            flat = "p k n -> p (k n)"
            load(ident, "c_ident", "consts_in")
            load(uqT.rearrange(flat.replace("k", "h")), "uqT", "absorb_in")
            load(ukT.rearrange(flat.replace("k", "h")), "ukT", "absorb_in")
            load(uvT.rearrange(flat.replace("k", "h")), "uvT", "absorb_in")
            load(xo.rearrange(flat.replace("k", "h")), "xo", "absorb_in")
            load(wkvc.rearrange(flat), "wkvc", "cross_in")
            load(wkr.rearrange(flat), "wkr", "cross_in")
            load(wdq.rearrange(flat), "wdq", "cross_in")
            sp.dma_start(wqr[0:QK], d["wqr"].rearrange("p (k n) -> p k n", k=2)).then_inc(s["cross_in"], 16)
            load(keys, "c_keys", "cross_in")
            load(qtab.rearrange(flat), "c_qtab", "cross_in")
            load(ktab.rearrange(flat), "c_ktab", "cross_in")
            load(w1.rearrange(flat), "w1", "front_in")
            load(w2[:, 0, :], "w2a", "front_in")
            load(w2[0:DMIX, 1, :], "w2b", "front_in")
            load(maa.rearrange(flat), "maa", "front_in")
            load(dw1.rearrange(flat), "dw1", "front_in")
            load(dw2[0:DDEC + 1], "dw2", "front_in")
            load(bonus, "bonus", "front_in")
            load(gam, "gam", "front_in")
            load(bet, "bet", "front_in")
            for w, n in ((wk, "wk"), (wv, "wv"), (wr, "wr"), (wg, "wg")):
                load(w.rearrange(flat), n, "proj_in")
            load(gap.rearrange(flat), "c_gap", "proj_in")
            load(pick_wide, "c_pick", "consts_in")
            load(wo.rearrange(flat), "wo", "proj_in")
            load(before[:].rearrange("p a n -> p (a n)"), "c_before", "router_in")
            load(router[:].rearrange("p k e -> p (k e)"), "router", "router_in")
            load(iota_e[:], "c_iota", "router_in")
            load(taken[:], "c_first", "router_in")
            load(first_row[:], "c_first", "router_in")
            load(steps[:], "c_steps", "router_in")
            sp.wait_ge(s["absorb_done"], 3 * XH)
            sp.wait_ge(s["ident_bf_set"], 2)

            def loads(i):
                after(sp, "x1_ready", i * HALF)
                sp.dma_start(x_in[:], d["x"][i]).then_inc(s["x_in_loaded"], 16)
                after(sp, "qlat_mm", i)
                sp.dma_start(ctxT.rearrange(flat), d["ctxT"][i]).then_inc(s["ctx_in"], 16)
                after(sp, "seg_float", i)
                sp.dma_start(segi.bitcast(I32), d["seg"][i]).then_inc(s["seg_in"], 16)

            def store(i):
                sp.wait_ge(s["x2_ready"], (i + 1) * HALF)
                sp.dma_start(x2_dram[i], x1[:]).then_inc(s["x2_stored"], 16)

            loads(0)
            loads(1)
            store(0)
            with sp.Fori(1, B - 1) as i:
                loads(i + 1)
                store(i)
            store(B - 1)

            sp.wait_ge(s["x2_stored"], 16 * B)
            sp.wait_ge(s["scattered"], 16 * B * HALF * CHOICES)
            sp.wait_ge(s["table_ready"], 1)
            gu = 2 * KT * I
            for e in range(E):
                sp.dma_start(w_gu[:, e * gu:(e + 1) * gu], d["w_gate_up"][e]).then_inc(expert_in[e], 16)
                sp.dma_start(w_dn[:, e * IT * C:(e + 1) * IT * C], d["w_down"][e]).then_inc(expert_in[e], 16)
                if e == 0:
                    for n in range(E):
                        first = sp.value_load(count_int[0:1, n:n + 1], min_val=0, max_val=B * T)
                        sp.dma_start(xs[bass.ds(first + n * REGION, P), :], zeros).then_inc(s["padded"], 16)
                    sp.dma_start(xs[SPARE:SPARE + P, :], zeros).then_inc(s["padded"], 16)
                    sp.wait_ge(s["padded"], 16 * (E + 1))

                    for n in range(2):
                        row = sp.value_load(step_tab[0:1, 1, n:n + 1], min_val=0, max_val=SPARE)
                        sp.dma_start(m_x[n], xs[bass.ds(row, P), :]).then_inc(s[f"m_x_in_{n}"], 16)
            with sp.Fori(0, STEPS // 2) as pair:
                for n in range(2):
                    j = pair * 2 + n
                    row = sp.value_load(step_tab[0:1, 1, bass.ds(j + 2, 1)], min_val=0, max_val=SPARE)
                    sp.wait_ge(s["m_x_transposed"], j + 1)
                    sp.dma_start(m_x[n], xs[bass.ds(row, P), :]).then_inc(s[f"m_x_in_{n}"], 16)
                    sp.wait_ge(s["m_y_ready"], j + 1)
                    sp.dma_start(ys[bass.ds(j * P, P), :], m_y[n]).then_inc(s[f"m_y_stored_{n}"], 16)
            for n in range(NT):
                if n >= 3:
                    sp.wait_ge(s["summed"], n - 2)
                    sp.wait_ge(s[f"stored_{n % 3}"], 16 * (n // 3))
                sp.dma_start(res[n % 3], x2_dram[n // HALF][:, n % HALF, :]).then_inc(s[f"res_in_{n % 3}"], 16)
            for n in range(2):
                sp.wait_ge(s[f"m_x_in_{n}"], 16 * (STEPS // 2 + 1))
            for n in range(3):
                sp.wait_ge(s[f"stored_{n}"], 16 * len(range(n, NT, 3)))

        @block.tensor
        def _(pe):
            mm = nc.tensor.matmul

            def accumulate(dst, pairs):
                for n, (a, b) in enumerate(pairs):
                    last = mm(dst, a, b, start=(n == 0), stop=(n == len(pairs) - 1))
                return last

            pe.wait_ge(s["absorb_in"], 16 * 4)
            for h in range(XH):
                if h >= 2:
                    pe.wait_ge(s["absorb_done"], 3 * (h - 1))
                b = 4 * (h % 2)
                mm(ps[0:QK, b, 0:KVC], uqT[:, h, 0:QK], ukT[:, h, :], start=True, stop=True)
                mm(ps[0:QK, b, KVC:2 * KVC], uqT[:, h, QK:QC], ukT[:, h, :], start=True, stop=True)
                mm(ps[:, b + 1, :], uvT[:, h, :], xo[:, h, :], start=True, stop=True).then_inc(s["absorb_mm"], 1)
            pe.wait_ge(s["absorb_done"], 3 * XH)
            pe.wait_ge(s["consts_in"], 32)
            pe.wait_ge(s["cross_in"], 16 * 7)
            pe.wait_ge(s["front_in"], 16 * 9)
            pe.wait_ge(s["proj_in"], 16 * 6)
            pe.wait_ge(s["ones_set"], 3)
            pe.wait_ge(s["ident_bf_set"], 2)

            def latents(i):
                pe.wait_ge(s["ctx_in"], (i + 1) * 16)
                after(pe, "x2_ready", i * HALF)
                accumulate(ps[:, 6, 0:T], [(wkvc[:, k, :], ctxT[:, k, :]) for k in range(KT)])
                for h in range(HALF):
                    last = accumulate(ps[:, 6, T + h * P:T + (h + 1) * P],
                                      [(ctxT[:, k, h * P:(h + 1) * P], wkvc[:, k, :]) for k in range(KT)])
                last.then_inc(s["kvc_mm"], 1)

            def rotary_keys(i):
                pe.wait_ge(s["kvc_ready"], i + 1)
                pe.wait_ge(s["o_normed"], (i + 1) * KT)
                mm(ps[:, 7, 0:T], wkr[:, 0, :], kvcT, start=True, stop=True)
                mm(ps[:, 7, T:2 * T], wkr[:, 1, :], kvcT, start=True, stop=True).then_inc(s["kr_mm"], 1)

            def transposes(i, normed, src, b0, signal):
                for h in range(HALF):
                    pe.wait_ge(s[normed], i * HALF + h + 1)
                    for k in range(KT):
                        last = nc.tensor.transpose(ps[:, b0 + h, k * P:(k + 1) * P], src[:, h, k * P:(k + 1) * P], ident)
                    last.then_inc(s[signal], 1)

            pair_of = [ps[:, 2 * n:2 * n + 2, :].rearrange("p a (k n) -> p (a k) n", n=T) for n in range(4)]

            def low_rank(i):
                pe.wait_ge(s["xxx_ready"], i + 1)
                accumulate(ps[:, 4, 0:T], [(w1[:, k, 0:P], xxx[:, k, :]) for k in range(KT)])
                accumulate(ps[0:DMIX, 4, T:2 * T], [(w1[:, k, P:P + DMIX], xxx[:, k, :]) for k in range(KT)]).then_inc(s["z_mm"], 1)

            def mix(i, f):
                if f >= 2:
                    after(pe, "mix_used", i * MIX + f - 1)
                dst = pair_of[f % 2]
                for k in range(KT):
                    if f < 4:
                        rows = slice(DMIX * f, DMIX * (f + 1))
                        last = mm(dst[:, k, :], w2[rows, 0, k * P:(k + 1) * P], z_a[rows], start=True, stop=True, tile_position=(DMIX * f, 0))
                    else:
                        last = mm(dst[:, k, :], w2[0:DMIX, 1, k * P:(k + 1) * P], z_b[0:DMIX], start=True, stop=True)
                last.then_inc(s["mix_mm"], 1)

            def project(i, f, w, x, b, signal):
                pe.wait_ge(s["mixed_ready"], i * MIX + f + 1)
                for k in range(KT):
                    last = accumulate(pair_of[b][:, k, :], [(w[:, c, k * P:(k + 1) * P], x[:, c, :]) for c in range(KT)])
                last.then_inc(s[signal], 1)

            def time_mix(i):
                pe.wait_ge(s["z_ready"], i + 1)
                mix(i, 0)
                mix(i, 1)
                pe.wait_ge(s["mixed_ready"], i * MIX + 1)
                accumulate(ps[0:DDEC, 4, 0:T], [(dw1[:, k, :], mixed_x[0][:, k, :]) for k in range(KT)]).then_inc(s["zdec_mm"], 1)
                mix(i, 2)
                project(i, 1, wk, mixed_x[1], 3, "k_mm")
                pe.wait_ge(s["zdec_ready"], i + 1)
                after(pe, "taken_moved", i)
                for h in range(HALF):
                    last = mm(ps[:, 4 + h, :], z_dec[0:DDEC + 1, h * P:(h + 1) * P], dw2[0:DDEC + 1], start=True, stop=True)
                last.then_inc(s["dd_mm"], 1)
                mix(i, 3)
                after(pe, "mixed_ready", i * MIX + 3)
                pe.wait_ge(s["k_ready"], i + 1)
                for h in range(HALF):
                    last = accumulate(ps[:, 6 + h, :], [(mixed_x[0][:, k, h * P:(h + 1) * P], wv[:, k, :]) for k in range(KT)])
                last.then_inc(s["v_mm"], 1)
                mix(i, 4)
                pe.wait_ge(s["dd_capped"], i + 1)
                project(i, 3, wr, mixed_x[1], 2, "r_mm")
                pe.wait_ge(s["v_ready"], i + 1)
                project(i, 4, wg, mixed_x[0], 3, "g_mm")

            def gaps(i, k, halves=range(HALF)):
                for h in halves:
                    if k == 0 and h == 0:
                        pe.wait_ge(s["e_ready"], i + 1)
                        pe.wait_ge(s["mix_used"], (i + 1) * MIX)
                    after(pe, "decays_ready", i * 8 + 2 * k + h)
                    w = e_tok[:, h, k * P:(k + 1) * P]
                    mm(ps[:, 0, :], w, gap[:, h, 0:4 * P], start=True, stop=True)
                    mm(ps[:, 1, 0:3 * P], w, gap[:, h, 4 * P:7 * P], start=True, stop=True).then_inc(s["gap_mm"], 1)

            def grams(i, h):
                k, p = divmod(h, 2)
                rows = slice(HS * p, HS * (p + 1))
                at = (HS * p, 0)
                q = lev[k % 2]
                if p == 0:
                    pe.wait_ge(s["k_decayed"], i * KT + k + 1)
                    pe.wait_ge(s["r_decayed"], i * KT + k + 1)
                after(pe, "far_copied", i * RH + h)
                for t in range(HALF):
                    o = t * P
                    mm(ps[:, 5, o:o + P], q[rows, 5, o:o + P], q[rows, 5, o:o + P], start=True, stop=True, tile_position=at)
                    mm(ps[0:64, 5, T + 64 * t:T + 64 * t + 64], q[rows, 6, o:o + 64], q[rows, 6, o + 64:o + P],
                       start=True, stop=True, tile_position=at)
                mm(ps[:, 5, 3 * P:4 * P], q[rows, 0, 0:P], q[rows, 0, P:T], start=True, stop=True, tile_position=at).then_inc(s["gram_far"], 1)
                for b in range(3):
                    after(pe, "near_picked", i * (3 * RH) + (3 * h + b - 2 if h else 0))
                    for t in range(HALF):
                        o = slice(t * P, (t + 1) * P)
                        for n in range(2):
                            level = 2 * b + n - 1
                            left, right = ((kT[rows, k, o], ru[k % 2][rows, o]), (kT[rows, k, o], rT[rows, k, o]))[n] if b == 0 else (
                                q[rows, level, o], q[rows, level, o])
                            last = mm(ps[:, 2 + b, n * T + t * P:n * T + (t + 1) * P], left, right,
                                      start=True, stop=True, tile_position=at)
                    last.then_inc(s["gram_near"], 1)

            def values(i, h):
                k, p = divmod(h, 2)
                b = 6 + k % 2
                if h == 0:
                    pe.wait_ge(s["g_ready"], i + 1)
                if k >= 2 and p == 0:
                    after(pe, "o_normed", i * KT + k - 1)
                pe.wait_ge(s["near_picked"], i * (3 * RH) + 3 * (h + 1))
                v = [v_tok[:, t, h * HS:(h + 1) * HS] for t in range(HALF)]
                dst = [ps[:, b, t * P + p * HS:t * P + (p + 1) * HS] for t in range(HALF)]
                mm(dst[0], a_near[p][:, 0, :], v[0], start=True, stop=True)
                accumulate(dst[1], [(a_near[p][:, 1, :], v[1]), (a_far[p], v[0])]).then_inc(s["av_done"], 1)

            def output(i):
                pe.wait_ge(s["decays_ready"], (i + 1) * 8)
                for k in range(KT):
                    pe.wait_ge(s["o_normed"], i * KT + k + 1)
                    for t in range(HALF):
                        c = (k % 2) * T + t * P
                        last = nc.tensor.transpose(ps[:, k // 2, c:c + P], o_tok[:, t, k * P:(k + 1) * P], ident)
                    last.then_inc(s["o_transposed"], 1)
                pe.wait_ge(s["o_gated"], i + 1)
                for t in range(HALF):
                    accumulate(ps[:, 2 + t, :], [(oT[:, k, t * P:(t + 1) * P], wo[:, k, :]) for k in range(KT)]).then_inc(s["wo_mm"], 1)

            def query_latent(i):
                rotary_keys(i)
                pe.wait_ge(s["x1T_ready"], (i + 1) * HALF)
                for a in range(2):
                    last = accumulate(ps[0:QK, 6, a * T:(a + 1) * T], [(wdq[:, k, a * QK:(a + 1) * QK], x1T[:, k, :]) for k in range(KT)])
                last.then_inc(s["qlat_mm"], 1)
                pe.wait_ge(s["qlat_ready"], i + 1)
                pe.wait_ge(s["kr_ready"], i + 1)
                pe.wait_ge(s["bias_ready"], (i + 1) * HALF)

            UNITS = HALF * XH

            def head_query(i, u):
                t, h = divmod(u, XH)
                if u >= 2:
                    after(pe, "head_ready", i * UNITS + u - 1)
                q = q_lat[0:QK, :, t * P:(t + 1) * P]
                accumulate(ps[:, u % 2, 0:P], [(wqk[0:QK, a, h * KVC:(h + 1) * KVC], q[:, a, :]) for a in range(2)])
                for a in range(2):
                    last = mm(ps[:, u % 2, P:2 * P], wqr[0:QK, a, h * P:(h + 1) * P], q[:, a, :], start=(a == 0), stop=(a == 1))
                last.then_inc(s["head_mm"], 1)

            def scores(i, u):
                t = u // XH
                pe.wait_ge(s["head_ready"], i * UNITS + u + 1)
                if u >= 2:
                    after(pe, "exp_done", i * UNITS + u - 1)
                q, dst = q_head[u % 2], ps[:, 2 + u % 2, 0:T]
                mm(dst, q[:, 0, :], kvcT, start=True, stop=False)
                mm(dst, q[:, 1, :], krT, start=False, stop=False)
                mm(dst, ident_bf[:], bias[:, t, :], start=False, stop=True).then_inc(s["score_mm"], 1)

            def prob_transpose(i, u):
                pe.wait_ge(s["prob_ready"], i * UNITS + u + 1)
                if u >= 2:
                    after(pe, "probT_ready", i * UNITS + u - 1)
                for a in range(2):
                    last = nc.tensor.transpose(ps[:, 4 + u % 2, a * P:(a + 1) * P], prob[u % 3][:, a * P:(a + 1) * P], ident)
                last.then_inc(s["prob_transposed"], 1)

            def weigh(i, u):
                pe.wait_ge(s["probT_ready"], i * UNITS + u + 1)
                if u >= 1:
                    after(pe, "o_head_ready", i * UNITS + u)
                accumulate(ps[:, 6, 0:P], [(kvc[:, a, :], probT[u % 2][:, a, :]) for a in range(2)]).then_inc(s["pv_mm"], 1)

            def head_output(i, u):
                t, h = divmod(u, XH)
                pe.wait_ge(s["o_head_ready"], i * UNITS + u + 1)
                if h == 0:
                    after(pe, "x2_ready", i * HALF + t)
                mm(ps[:, 7, :], o_head[u % 2], wvo[:, h, :], start=(h == 0), stop=(h == XH - 1)).then_inc(s["out_mm"], 1)

            def route_logits(i):
                transposes(i, "ln3_normed", x3, 0, "x3_transposed")
                for h in range(HALF):
                    pe.wait_ge(s["x3T_ready"], i * HALF + h + 1)
                    last = accumulate(ps[:, 2, h * E:(h + 1) * E], [(x3T[:, k, h * P:(h + 1) * P], router[:, k, :]) for k in range(KT)])
                last.then_inc(s["logit_mm"], 1)

            def route_ranks(i):
                pe.wait_ge(s["both_ready"], i + 1)
                b = both[:].rearrange("p h e -> p (h e)")
                mm(ps[:, 5, 0:HALF * E], before[:, 0, :], b, start=True, stop=True)
                mm(ps[:, 5, HALF * E:2 * HALF * E], before[:, 1, :], b, start=True, stop=True).then_inc(s["rank_mm"], 1)

            def batch(i, last_one=None):
                transposes(i, "ln1_normed", xn, 2, "h_transposed")
                latents(i)
                low_rank(i)
                if last_one is not None:
                    route_logits(last_one)
                    route_ranks(last_one)
                time_mix(i)
                gaps(i, 0)
                for h in range(RH):
                    if h // 2 + 1 < KT:
                        gaps(i, h // 2 + 1, [h % 2])
                    grams(i, h)
                    if h >= 1:
                        values(i, h - 1)
                values(i, RH - 1)
                output(i)
                transposes(i, "ln2_normed", xn, 4, "x1_transposed")
                query_latent(i)
                head_query(i, 0)
                for u in range(UNITS + 2):
                    if u < UNITS:
                        scores(i, u)
                    if 1 <= u <= UNITS:
                        prob_transpose(i, u - 1)
                    if u + 1 < UNITS:
                        head_query(i, u + 1)
                    if 1 <= u <= UNITS:
                        weigh(i, u - 1)
                    if u >= 2:
                        head_output(i, u - 2)

            pe.wait_ge(s["router_in"], 16 * 6)
            batch(0)
            with pe.Fori(1, B) as i:
                batch(i, i - 1)
            pe.wait_ge(s["x2_ready"], B * HALF)
            route_logits(B - 1)
            route_ranks(B - 1)

            pe.wait_ge(s["table_ready"], 1)

            def take_tokens(j, n):
                pe.wait_ge(s[f"m_x_in_{n}"], (j - n) * 8 + 16)
                after(pe, "m_xT_ready", j)
                for k in range(KT):
                    last = nc.tensor.transpose(ps[:, 2 + n, k * P:(k + 1) * P], m_x[n][:, k * P:(k + 1) * P], ident)
                last.then_inc(s["m_x_transposed"], 1)

            def gate_up(j, n):
                e = pe.value_load(step_tab[0:1, 0, bass.ds(j, 1)], min_val=0, max_val=E - 1)
                pe.wait_ge(s["expert_ready"], e + 1)
                pe.wait_ge(s["m_xT_ready"], j + 1)
                after(pe, "m_h_ready", j)
                for a in range(2):
                    last = accumulate(ps[:, a, 0:I], [(m_xT[n][:, k, :], w_gu[:, bass.ds(e * (2 * KT * I) + (a * KT + k) * I, I)])
                                                      for k in range(KT)])
                    last.then_inc(s["gate_mm" if a == 0 else "up_mm"], 1)

            def turn_inner(j):
                pe.wait_ge(s["m_h_ready"], j + 1)
                after(pe, "m_hT_ready", j)
                for a, (o, m) in enumerate(INNER):
                    last = nc.tensor.transpose(ps[0:m, 4, a * P:(a + 1) * P], m_h[:, o:o + m], ident)
                last.then_inc(s["m_h_transposed"], 1)

            def down(j, n):
                e = pe.value_load(step_tab[0:1, 0, bass.ds(j, 1)], min_val=0, max_val=E - 1)
                pe.wait_ge(s["m_hT_ready"], j + 1)
                if n == 1 or not isinstance(j, int):
                    after(pe, "m_y_ready", j - 1)
                accumulate(ps[:, 5 + n, :], [(m_hT[n][0:m, a, :], w_dn[0:m, bass.ds(e * (IT * C) + a * C, C)])
                                             for a, (o, m) in enumerate(INNER)]).then_inc(s["down_mm"], 1)

            take_tokens(0, 0)
            gate_up(0, 0)
            take_tokens(1, 1)
            turn_inner(0)
            gate_up(1, 1)
            take_tokens(2, 0)
            down(0, 0)
            turn_inner(1)
            with pe.Fori(1, STEPS // 2) as pair:
                for n in range(2):
                    j = pair * 2 + n
                    gate_up(j, n)
                    take_tokens(j + 1, 1 - n)
                    down(j - 1, 1 - n)
                    turn_inner(j)
            down(STEPS - 1, 1)

        @block.scalar
        def _(act):
            fn = nc.scalar.activation

            for h in range(XH):
                act.wait_ge(s["absorb_mm"], h + 1)
                b = 4 * (h % 2)
                for a in range(2):
                    nc.scalar.copy(wqk[0:QK, a, h * KVC:(h + 1) * KVC], ps[0:QK, b, a * KVC:(a + 1) * KVC]).then_inc(s["absorb_done"], 1)
                nc.scalar.copy(wvo[:, h, :], ps[:, b + 1, :]).then_inc(s["absorb_done"], 1)

            def latents(i):
                act.wait_ge(s["kvc_mm"], i + 1)
                nc.scalar.copy(kvcT, ps[:, 6, 0:T])
                nc.scalar.copy(kvc.rearrange("p k n -> p (k n)"), ps[:, 6, T:2 * T]).then_inc(s["kvc_ready"], 1)

            def take_transposed(i, signal_in, dst, b0, signal):
                for h in range(HALF):
                    act.wait_ge(s[signal_in], i * HALF + h + 1)
                    nc.scalar.copy(dst[:, :, h * P:(h + 1) * P], ps[:, b0 + h, :].rearrange("p (k n) -> p k n", k=KT)).then_inc(s[signal], 1)

            def pair_of(n):
                return ps[:, 2 * n:2 * n + 2, :].rearrange("p a (k n) -> p (a k) n", n=T)

            def squash_low_rank(i):
                act.wait_ge(s["z_mm"], i + 1)
                fn(z_a, ps[:, 4, 0:T], ACT.Tanh)
                fn(z_b[0:DMIX], ps[0:DMIX, 4, T:2 * T], ACT.Tanh).then_inc(s["z_ready"], 1)

            def time_mix(i):
                act.wait_ge(s["zdec_mm"], i + 1)
                fn(z_dec[0:DDEC], ps[0:DDEC, 4, 0:T], ACT.Tanh).then_inc(s["zdec_ready"], 1)
                act.wait_ge(s["k_mm"], i + 1)
                nc.scalar.copy(kT[:], pair_of(3)).then_inc(s["k_ready"], 1)
                act.wait_ge(s["dd_capped"], i + 1)
                fn(e_tok[:], e_tok[:], ACT.Exp).then_inc(s["e_ready"], 1)
                act.wait_ge(s["v_mm"], i + 1)
                after(act, "scattered", i * (16 * HALF * CHOICES))
                nc.scalar.copy(v_tok[:], ps[:, 6:8, :]).then_inc(s["v_ready"], 1)
                act.wait_ge(s["r_mm"], i + 1)
                nc.scalar.copy(rT[:], pair_of(2)).then_inc(s["r_ready"], 1)
                act.wait_ge(s["g_mm"], i + 1)
                fn(half_gate.rearrange("p h (k n) -> p (h k) n", n=T), pair_of(3), ACT.Tanh, scale=0.5).then_inc(s["g_tanh"], 1)

            def decays(i, k, halves=range(HALF)):
                q = lev[k % 2]
                if k >= 2:
                    after(act, "gram_near", i * (3 * RH) + 6 * (k - 1))
                for h in halves:
                    act.wait_ge(s["gap_mm"], i * 8 + 2 * k + h + 1)
                    o = slice(h * P, (h + 1) * P)
                    fn(q[:, 0:4, o], ps[:, 0, :].rearrange("p (l n) -> p l n", l=4), ACT.Exp)
                    fn(q[:, 4:7, o], ps[:, 1, 0:3 * P].rearrange("p (l n) -> p l n", l=3), ACT.Exp).then_inc(s["decays_ready"], 1)

            def far(i, h):
                p = h % 2
                act.wait_ge(s["gram_far"], i * RH + h + 1)
                if h >= 2:
                    after(act, "av_done", i * RH + h - 1)
                near = ps[:, 5, 0:T].rearrange("p (t n) -> p t n", t=HALF)
                nc.scalar.copy(a_near[p][0:32, :, 32:64], near[0:32, :, 32:64])
                nc.scalar.copy(a_near[p][64:96, :, 96:128], near[64:96, :, 96:128])
                nc.scalar.copy(a_near[p][0:64, :, 64:128], ps[0:64, 5, T:T + P].rearrange("p (t n) -> p t n", t=HALF))
                nc.scalar.copy(a_far[p], ps[:, 5, 3 * P:4 * P]).then_inc(s["far_copied"], 1)

            def affine(i):
                for k in range(KT):
                    after(act, "o_transposed", i * KT + (k // 2 + 1) * 2)
                    c = (k % 2) * T
                    fn(oT[:, k, :], ps[:, k // 2, c:c + T], ACT.Identity, scale=gam[:, k:k + 1], bias=bet[:, k:k + 1]).then_inc(s["o_affine"], 1)

            def query_latent(i):
                act.wait_ge(s["qlat_mm"], i + 1)
                nc.scalar.copy(q_lat[0:QK], ps[0:QK, 6, :].rearrange("p (a n) -> p a n", a=2)).then_inc(s["qlat_ready"], 1)

            UNITS = HALF * XH

            def exponentials(i, u):
                act.wait_ge(s["max_ready"], i * UNITS + u + 1)
                if u >= 3:
                    after(act, "prob_transposed", i * UNITS + u - 2)
                if u >= 4:
                    after(act, "sum_inverted", i * UNITS + u - 3)
                fn(prob[u % 3], ps[:, 2 + u % 2, 0:T], ACT.Exp, bias=negmax[:, u % 4:u % 4 + 1],
                   accum_out=psumr[:, u % 4:u % 4 + 1]).then_inc(s["exp_done"], 1)

            def prob_back(i, u):
                act.wait_ge(s["prob_transposed"], i * UNITS + u + 1)
                if u >= 2:
                    after(act, "pv_mm", i * UNITS + u - 1)
                nc.scalar.copy(probT[u % 2][:], ps[:, 4 + u % 2, 0:T].rearrange("p (a n) -> p a n", a=2)).then_inc(s["probT_ready"], 1)

            def o_back(i, u):
                act.wait_ge(s["pv_mm"], i * UNITS + u + 1)
                if u >= 2:
                    after(act, "out_mm", i * UNITS + u - 1)
                nc.scalar.copy(o_head[u % 2], ps[:, 6, 0:P]).then_inc(s["o_head_ready"], 1)

            def route(i):
                for h in range(HALF):
                    act.wait_ge(s["x3_transposed"], i * HALF + h + 1)
                    nc.scalar.copy(x3T[:, :, h * P:(h + 1) * P], ps[:, h, :].rearrange("p (k n) -> p k n", k=KT)).then_inc(s["x3T_ready"], 1)
                act.wait_ge(s["gap12"], i + 1)
                fn(odds[:, 1, :], odds[:, 0, :], ACT.Exp).then_inc(s["odds_ready"], 1)

            def batch(i, last_one=None):
                take_transposed(i, "h_transposed", hT[:, :, 1:T + 1], 2, "h_ready")
                latents(i)
                squash_low_rank(i)
                if last_one is not None:
                    route(last_one)
                time_mix(i)
                decays(i, 0)
                for h in range(RH):
                    if h // 2 + 1 < KT:
                        decays(i, h // 2 + 1, [h % 2])
                    far(i, h)
                affine(i)
                take_transposed(i, "x1_transposed", x1T, 4, "x1T_ready")
                query_latent(i)
                for u in range(UNITS + 1):
                    if u >= 1:
                        prob_back(i, u - 1)
                    if u < UNITS:
                        exponentials(i, u)
                    if u >= 1:
                        o_back(i, u - 1)

            act.wait_ge(s["front_in"], 16 * 9)
            act.wait_ge(s["ones_set"], 3)
            batch(0)
            with act.Fori(1, B) as i:
                batch(i, i - 1)
            route(B - 1)

            def take_tokens(j, n):
                act.wait_ge(s["m_x_transposed"], j + 1)
                if n == 1 or not isinstance(j, int):
                    after(act, "gate_mm", j - 1)
                    after(act, "up_mm", j - 1)
                nc.scalar.copy(m_xT[n][:], ps[:, 2 + n, :].rearrange("p (k n) -> p k n", k=KT)).then_inc(s["m_xT_ready"], 1)

            def squash(j):
                act.wait_ge(s["gate_mm"], j + 1)
                after(act, "m_silued", j)
                fn(m_tanh, ps[:, 0, 0:I], ACT.Tanh, scale=0.5).then_inc(s["m_tanhed"], 1)

            def turn_inner(j, n):
                act.wait_ge(s["m_h_transposed"], j + 1)
                if n == 1 or not isinstance(j, int):
                    after(act, "down_mm", j - 1)
                nc.scalar.copy(m_hT[n][:, 0:2, :], ps[:, 4, 0:2 * P].rearrange("p (k n) -> p k n", k=2))
                nc.scalar.copy(m_hT[n][0:INNER[2][1], 2, :], ps[0:INNER[2][1], 4, 2 * P:3 * P]).then_inc(s["m_hT_ready"], 1)

            take_tokens(0, 0)
            squash(0)
            take_tokens(1, 1)
            turn_inner(0, 0)
            squash(1)
            take_tokens(2, 0)
            turn_inner(1, 1)
            with act.Fori(1, STEPS // 2) as pair:
                for n in range(2):
                    j = pair * 2 + n
                    squash(j)
                    take_tokens(j + 1, 1 - n)
                    turn_inner(j, n)
            for n in range(NT):
                act.wait_ge(s["summed"], n + 1)
                act.dma_start(out[n // HALF, (n % HALF) * P:(n % HALF + 1) * P, :], res[n % 3]).then_inc(s[f"stored_{n % 3}"], 16)

        @block.vector
        def _(dve):
            ts, tt, stt = nc.vector.tensor_scalar, nc.vector.tensor_tensor, nc.vector.scalar_tensor_tensor

            def norm_stats(i, ln, src):
                st, mv = (st1, mv1) if ln == "ln1" else (st23, mv23)
                for h in range(HALF):
                    nc.vector.bn_stats(st[:, h, :], src[:, h, :]).then_inc(s[ln + "_raw"], 1)
                for h in range(HALF):
                    wait_apart(dve, ln + "_raw", i * HALF + h + 1)
                    nc.vector.bn_aggr(mv[:, h, :], st[:, h, :]).then_inc(s[ln + "_stats"], 1)

            def normalise(i, ln, src, dst=xn):
                mv, rstd = (mv1, rstd1) if ln == "ln1" else (mv23, rstd23)
                for h in range(HALF):
                    dve.wait_ge(s[ln + "_rstd"], i * HALF + h + 1)
                    ts(dst[:, h, :], src[:, h, :], mv[:, h, 0:1], rstd[:, h:h + 1], ALU.subtract, ALU.mult).then_inc(s[ln + "_normed"], 1)

            def shift_mix(i):
                dve.wait_ge(s["h_ready"], (i + 1) * HALF)
                tt(xx[:], hT[:, :, 0:T], hT[:, :, 1:T + 1], ALU.subtract).then_inc(s["xx_ready"], 1)
                dve.wait_ge(s["xx_ready"], i + 1)
                for k in range(KT):
                    last = stt(out=xxx[:, k, :], in0=xx[:, k, :], scalar=maa[:, 0, k:k + 1], in1=hT[:, k, 1:T + 1], op0=ALU.mult, op1=ALU.add)
                last.then_inc(s["xxx_ready"], 1)

            def pair_of(n):
                return ps[:, 2 * n:2 * n + 2, :].rearrange("p a (k n) -> p (a k) n", n=T)

            def mixed(i, f):
                dve.wait_ge(s["mix_mm"], i * MIX + f + 1)
                if f == 2:
                    dve.wait_ge(s["zdec_mm"], i + 1)
                if f == 3:
                    dve.wait_ge(s["k_mm"], i + 1)
                if f == 4:
                    dve.wait_ge(s["v_mm"], i + 1)
                for k in range(KT):
                    last = stt(out=mixed_x[f % 2][:, k, :], in0=pair_of(f % 2)[:, k, :], scalar=maa[:, f + 1, k:k + 1],
                               in1=xx[:, k, :], op0=ALU.add, op1=ALU.mult)
                last.then_inc(s["mix_used"], 1)

            def time_mix(i):
                mixed(i, 2)
                dve.wait_ge(s["dd_mm"], i + 1)
                ts(e_tok[:], ps[:, 4:6, :], DECAY_CAP, None, ALU.min).then_inc(s["dd_capped"], 1)
                mixed(i, 3)
                mixed(i, 4)
                dve.wait_ge(s["g_tanh"], i + 1)
                stt(out=gT[:], in0=half_gate.rearrange("p h (k n) -> p (h k) n", n=T), scalar=1.0, in1=pair_of(3),
                    op0=ALU.add, op1=ALU.mult).then_inc(s["g_ready"], 1)

            def decay_queries(i, k):
                after(dve, "decays_ready", i * 8 + 2 * k + 2)
                dve.wait_ge(s["r_ready"], i + 1)
                q = lev[k % 2]
                for slot in range(7):
                    half = 1 << (slot or 7)
                    upper = q[:, slot, :].rearrange("p (n two h) -> p n two h", two=2, h=half)[:, :, 1, :]
                    r = rT[:, k, :].rearrange("p (n two h) -> p n two h", two=2, h=half)[:, :, 1, :]
                    last = tt(upper, upper, r, ALU.mult)
                last.then_inc(s["r_decayed"], 1)

            def pick_near(i, h):
                wait_apart(dve, "far_copied", i * RH + h + 1)
                a = a_near[h % 2].rearrange("p t n -> p (t n)")
                for n in range(6):
                    if n % 2 == 0:
                        wait_apart(dve, "gram_near", i * (3 * RH) + 3 * h + n // 2 + 1)
                        if n:
                            wait_apart(dve, "near_picked", i * (3 * RH) + 3 * h + n // 2)
                    else:
                        wait_apart(dve, "level_picked", (i * RH + h) * 3 + n // 2 + 1)
                    nc.vector.copy_predicated(a, pick[:, n, :], ps[:, 2 + n // 2, (n % 2) * T:(n % 2 + 1) * T]
                                              ).then_inc(s["near_picked" if n % 2 else "level_picked"], 1)

            def group_stats(i, k):
                after(dve, "av_done", i * RH + 2 * k + 2)
                b = 6 + k % 2
                for n in range(4):
                    last = nc.vector.bn_stats(gst[:, k % 2, 6 * n:6 * n + 6], ps[:, b, n * HS:(n + 1) * HS])
                last.then_inc(s["gn_raw"], 1)
                wait_apart(dve, "gn_raw", i * KT + k + 1)
                for n in range(4):
                    last = nc.vector.bn_aggr(gmv[:, k % 2, 2 * n:2 * n + 2], gst[:, k % 2, 6 * n:6 * n + 6])
                last.then_inc(s["gn_stats"], 1)

            def group_norm(i, k):
                dve.wait_ge(s["gn_rstd"], i * KT + k + 1)
                b = 6 + k % 2
                for n in range(4):
                    t, p = divmod(n, 2)
                    last = ts(o_tok[:, t, k * P + p * HS:k * P + (p + 1) * HS], ps[:, b, n * HS:(n + 1) * HS],
                              gmv[:, k % 2, 2 * n:2 * n + 1], grstd[:, k % 2, n:n + 1], ALU.subtract, ALU.mult)
                last.then_inc(s["o_normed"], 1)

            def gate_and_add(i):
                dve.wait_ge(s["o_affine"], (i + 1) * KT)
                tt(oT[:], oT[:], gT[:], ALU.mult).then_inc(s["o_gated"], 1)
                after(dve, "x2_stored", i * 16)
                for h in range(HALF):
                    dve.wait_ge(s["wo_mm"], i * HALF + h + 1)
                    stt(out=x1[:, h, :], in0=ps[:, 2 + h, :], scalar=0.5, in1=x_in[:, h, :], op0=ALU.mult, op1=ALU.add).then_inc(s["x1_ready"], 1)

            def rotary_keys(i):
                dve.wait_ge(s["kr_mm"], i + 1)
                tt(kr_tmp, ps[:, 7, 0:T], ktab[:, 0, :], ALU.mult).then_inc(s["kr_cos"], 1)
                tt(krT, ps[:, 7, T:2 * T], ktab[:, 1, :], ALU.mult).then_inc(s["kr_sin"], 1)
                dve.wait_ge(s["kr_cos"], i + 1)
                dve.wait_ge(s["kr_sin"], i + 1)
                tt(krT, krT, kr_tmp, ALU.add).then_inc(s["kr_ready"], 1)

            def window(i):
                dve.wait_ge(s["seg_in"], (i + 1) * 16)
                nc.vector.tensor_copy(segf, segi.bitcast(I32)).then_inc(s["seg_float"], 1)
                dve.wait_ge(s["seg_float"], i + 1)
                for h in range(HALF):
                    n = i * HALF + h + 1
                    ts(late, keys, segf[:, h:h + 1], 0.0, ALU.subtract, ALU.is_gt).then_inc(s["late_set"], 1)
                    ts(early, keys, segf[:, h:h + 1], -float(LOOKBACK), ALU.subtract, ALU.is_lt).then_inc(s["early_set"], 1)
                    dve.wait_ge(s["late_set"], n)
                    dve.wait_ge(s["early_set"], n)
                    tt(late, late, early, ALU.add).then_inc(s["bad_set"], 1)
                    dve.wait_ge(s["bad_set"], n)
                    ts(bias[:, h, :], late, NEG, None, ALU.mult).then_inc(s["bias_ready"], 1)
                    dve.wait_ge(s["bias_ready"], n)

            UNITS = HALF * XH

            def head_query(i, u):
                dve.wait_ge(s["head_mm"], i * UNITS + u + 1)
                if u >= 2:
                    after(dve, "score_mm", i * UNITS + u - 1)
                tt(q_head[u % 2].rearrange("p a n -> p (a n)"), ps[:, u % 2, 0:2 * P], qtab[:, u // XH, :], ALU.mult).then_inc(s["head_ready"], 1)

            def row_max(i, u):
                dve.wait_ge(s["score_mm"], i * UNITS + u + 1)
                if u >= 4:
                    after(dve, "exp_done", i * UNITS + u - 3)
                nc.vector.tensor_reduce(negmax[:, u % 4:u % 4 + 1], ps[:, 2 + u % 2, 0:T], AX.X, ALU.max, negate=True).then_inc(s["max_ready"], 1)

            def divide(i, u):
                dve.wait_ge(s["exp_done"], i * UNITS + u + 1)
                nc.vector.reciprocal(prec[:, u % 4:u % 4 + 1], psumr[:, u % 4:u % 4 + 1]).then_inc(s["sum_inverted"], 1)
                dve.wait_ge(s["sum_inverted"], i * UNITS + u + 1)
                ts(prob[u % 3], prob[u % 3], prec[:, u % 4:u % 4 + 1], None, ALU.mult).then_inc(s["prob_ready"], 1)

            def add_cross(i, h):
                after(dve, "out_mm", i * UNITS + (h + 1) * XH)
                tt(x1[:, h, :], ps[:, 7, :], x1[:, h, :], ALU.add).then_inc(s["x2_ready"], 1)

            weights_of = weights[:].rearrange("p (n k) -> p n k", k=CHOICES)

            def route_norm(i):
                dve.wait_ge(s["x2_ready"], (i + 1) * HALF)
                norm_stats(i, "ln3", x1)
                normalise(i, "ln3", x1, x3)

            def route_choose(i):
                dve.wait_ge(s["logit_mm"], i + 1)
                nc.vector.tensor_copy(logit[:].rearrange("p h e -> p (h e)"), ps[:, 2, 0:HALF * E]).then_inc(s["route_link"], 1)
                wait_apart(dve, "route_link", i * 10 + 1)
                for h in range(HALF):
                    last = nc.vector.max(top[:, h, :], logit[:, h, :])
                last.then_inc(s["route_link"], 1)
                wait_apart(dve, "route_link", i * 10 + 2)
                for h in range(HALF):
                    last = nc.vector.max_index(topi[:, h, :], top[:, h, :], logit[:, h, :])
                last.then_inc(s["topi_ready"], 1)
                tt(odds[:, 0, :], top[:, :, 1], top[:, :, 0], ALU.subtract).then_inc(s["gap12"], 1)
                dve.wait_ge(s["topi_ready"], i + 1)
                nc.vector.tensor_copy(topf[:], topi[:]).then_inc(s["route_link"], 1)
                after(dve, "route_link", i * 10 + 3)
                for h in range(HALF):
                    for k in range(CHOICES):
                        last = ts(hot[:, h, k, :], iota_e[:], topf[:, h, k:k + 1], 1.0, ALU.is_equal, ALU.mult)
                last.then_inc(s["route_link"], 1)
                after(dve, "route_link", i * 10 + 4)
                tt(both[:], hot[:, :, 0, :], hot[:, :, 1, :], ALU.add).then_inc(s["both_ready"], 1)
                dve.wait_ge(s["odds_ready"], i + 1)
                ts(odds[:, 2, :], odds[:, 1, :], 1.0, 2.0, ALU.add, ALU.mult).then_inc(s["route_link"], 1)
                after(dve, "route_link", i * 10 + 5)
                nc.vector.reciprocal(odds[:, 2, :], odds[:, 2, :]).then_inc(s["route_link"], 1)
                wait_apart(dve, "route_link", i * 10 + 6)
                tt(weights_of[:, bass.ds(i * HALF, HALF), 1], odds[:, 2, :], odds[:, 1, :], ALU.mult)
                nc.vector.tensor_copy(weights_of[:, bass.ds(i * HALF, HALF), 0], odds[:, 2, :]).then_inc(s["w_kept"], 1)

            def route_place(i):
                dve.wait_ge(s["rank_mm"], i + 1)
                for h in range(HALF):
                    last = tt(place[:, h, :], ps[:, 5, h * E:(h + 1) * E], taken[:], ALU.add)
                last.then_inc(s["route_link"], 1)
                after(dve, "route_link", i * 10 + 7)
                tt(taken[:], ps[:, 5, HALF * E:HALF * E + E], taken[:], ALU.add)
                tt(place[:, 1, :], ps[:, 5, HALF * E:HALF * E + E], place[:, 1, :], ALU.add).then_inc(s["route_link"], 1)
                after(dve, "route_link", i * 10 + 8)
                tt(taken[:], ps[:, 5, HALF * E + E:HALF * E + 2 * E], taken[:], ALU.add).then_inc(s["taken_moved"], 1)
                for h in range(HALF):
                    for k in range(CHOICES):
                        last = tt(picked[:, h, k, :], hot[:, h, k, :], place[:, h, :], ALU.mult)
                last.then_inc(s["route_link"], 1)
                after(dve, "route_link", i * 10 + 9)
                nc.vector.tensor_reduce(slotf[:], picked[:].rearrange("p h k e -> p (h k) e"), AX.X, ALU.add).then_inc(s["route_link"], 1)
                after(dve, "route_link", i * 10 + 10)
                after(dve, "scattered", i * (16 * HALF * CHOICES))
                nc.vector.tensor_copy(slot[:], slotf[:]).then_inc(s["slot_ready"], 1)
                nc.vector.tensor_copy(slots[:, bass.ds(i * (HALF * CHOICES), HALF * CHOICES)], slotf[:])
                nc.vector.tensor_copy(experts_of[:].rearrange("p (n k) -> p n k", k=CHOICES)[:, bass.ds(i * HALF, HALF), :],
                                      topf[:, :, 0:CHOICES]).then_inc(s["slots_kept"], 1)

            def step_table():
                links = [0]

                def link(ins):
                    links[0] += 1
                    ins.then_inc(s["table_link"], 1)
                    dve.wait_ge(s["table_link"], links[0])

                link(tt(is_past[:, 0:E], taken[:], first_row[:], ALU.subtract))
                link(nc.vector.tensor_copy(count_int[:], is_past[:, 0:E]))
                link(ts(n_int[:], is_past[:, 0:E], float(P - 1), None, ALU.add))
                link(ts(n_int[:], n_int[:], 7, None, ALU.arith_shift_right))
                link(nc.vector.tensor_copy(n_tiles[:], n_int[:]))
                link(nc.vector.tensor_copy(ends[:, 0, 0:1], n_tiles[:, 0:1]))
                for e in range(1, E):
                    link(tt(ends[:, 0, e:e + 1], ends[:, 0, e - 1:e], n_tiles[:, e:e + 1], ALU.add))
                link(nc.vector.memset(step_e, 0.0))
                link(nc.vector.memset(step_row, 0.0))
                for e in range(E):
                    ts(is_past, steps[:], ends[:, 0, e:e + 1], 1.0, ALU.is_ge, ALU.mult)
                    link(ts(past_tiles, steps[:], ends[:, 0, e:e + 1], n_tiles[:, e:e + 1], ALU.is_ge, ALU.mult))
                    tt(step_e, step_e, is_past, ALU.add)
                    link(tt(step_row, step_row, past_tiles, ALU.add))
                link(tt(step_row, steps[:], step_row, ALU.subtract))
                link(ts(is_past, step_e, float(REGION), None, ALU.mult))
                link(stt(out=step_row, in0=step_row, scalar=float(P), in1=is_past, op0=ALU.mult, op1=ALU.add))
                ts(step_tab[:, 0, :], step_e, float(E - 1), None, ALU.min)
                link(ts(step_tab[:, 1, :], step_row, float(SPARE), None, ALU.min))
                link(tt(ends[:, 1, :], ends[:, 0, :], n_tiles[:], ALU.subtract))
                link(stt(out=ends[:, 1, :], in0=ends[:, 1, :], scalar=float(P), in1=first_row[:], op0=ALU.mult, op1=ALU.subtract))
                dve.wait_ge(s["slots_kept"], B)
                shape = [P, NT * CHOICES, E]
                link(tt(chosen, experts_of[:].unsqueeze(2).to_broadcast(shape), iota_e[:].unsqueeze(1).to_broadcast(shape), ALU.is_equal))
                link(tt(chosen, chosen, ends[:, 1, :].unsqueeze(1).to_broadcast(shape), ALU.mult))
                link(nc.vector.tensor_reduce(moved, chosen, AX.X, ALU.add))
                link(tt(rows[:], slots[:], moved, ALU.add))
                nc.vector.memset(zeros, 0.0).then_inc(s["table_ready"], 1)
                dve.wait_ge(s["table_ready"], 1)

            dve.wait_ge(s["absorb_done"], 3 * XH)
            dve.wait_ge(s["router_in"], 16 * 6)
            dve.wait_ge(s["consts_in"], 32)
            nc.vector.tensor_copy(ident_bf[:], ident).then_inc(s["ident_bf_set"], 1)
            nc.vector.tensor_copy(pick.rearrange("p l n -> p (l n)"), pick_wide).then_inc(s["ident_bf_set"], 1)
            dve.wait_ge(s["ident_bf_set"], 2)
            dve.wait_ge(s["front_in"], 16 * 9)
            dve.wait_ge(s["cross_in"], 16 * 7)
            dve.wait_ge(s["proj_in"], 16 * 6)
            dve.wait_ge(s["ones_set"], 3)

            def first_norm(i):
                dve.wait_ge(s["x_in_loaded"], (i + 1) * 16)
                after(dve, "x1_transposed", i * HALF)
                norm_stats(i, "ln1", x_in)
                normalise(i, "ln1", x_in)

            def batch(i, last_one=None, next_one=None):
                shift_mix(i)
                if last_one is not None:
                    route_norm(last_one)
                    route_choose(last_one)
                mixed(i, 0)
                mixed(i, 1)
                if last_one is not None:
                    route_place(last_one)
                time_mix(i)
                decay_queries(i, 0)
                for h in range(RH):
                    k = h // 2
                    if h % 2 == 0 and k + 1 < KT:
                        decay_queries(i, k + 1) if k else None
                    pick_near(i, h)
                    if h == 0:
                        decay_queries(i, 1)
                    if h >= 2 and h % 2 == 0:
                        group_stats(i, k - 1)
                    if h >= 3 and h % 2 == 1:
                        group_norm(i, k - 1)
                group_stats(i, KT - 1)
                group_norm(i, KT - 1)
                gate_and_add(i)
                dve.wait_ge(s["x1_ready"], (i + 1) * HALF)
                norm_stats(i, "ln2", x1)
                window(i)
                normalise(i, "ln2", x1)
                rotary_keys(i)
                head_query(i, 0)
                for u in range(UNITS + 2):
                    if u < UNITS:
                        row_max(i, u)
                    if u + 1 < UNITS:
                        head_query(i, u + 1)
                    if u < UNITS:
                        divide(i, u)
                    if u == 4 and next_one is not None:
                        first_norm(next_one)
                    if u - 2 in (XH - 1, UNITS - 1):
                        add_cross(i, (u - 2) // XH)

            first_norm(0)
            batch(0, None, 1)
            with dve.Fori(1, B - 1) as i:
                batch(i, i - 1, i + 1)
            batch(B - 1, B - 2)
            route_norm(B - 1)
            route_choose(B - 1)
            route_place(B - 1)
            step_table()

            def inner(j):
                dve.wait_ge(s["m_tanhed"], j + 1)
                stt(out=m_silu, in0=m_tanh, scalar=1.0, in1=ps[:, 0, 0:I], op0=ALU.add, op1=ALU.mult).then_inc(s["m_silued"], 1)
                dve.wait_ge(s["up_mm"], j + 1)
                after(dve, "m_h_transposed", j)
                dve.wait_ge(s["m_silued"], j + 1)
                tt(m_h, m_silu, ps[:, 1, 0:I], ALU.mult).then_inc(s["m_h_ready"], 1)

            def finish(j, n):
                dve.wait_ge(s["down_mm"], j + 1)
                if not isinstance(j, int) or j >= 2:
                    after(dve, f"m_y_stored_{n}", (j - n) * 8)
                nc.vector.tensor_copy(m_y[n], ps[:, 5 + n, :]).then_inc(s["m_y_ready"], 1)

            inner(0)
            inner(1)
            finish(0, 0)
            with dve.Fori(1, STEPS // 2) as pair:
                for n in range(2):
                    j = pair * 2 + n
                    inner(j)
                    finish(j - 1, 1 - n)
            finish(STEPS - 1, 1)

            for n in range(NT):
                a = res[n % 3]
                dve.wait_ge(s[f"res_in_{n % 3}"], 16 * (n // 3 + 1))
                dve.wait_ge(s[f"y_in_{n % 3}"], 16 * CHOICES * (n // 3 + 1))
                for k in range(CHOICES):
                    w = weights[:, n * CHOICES + k:n * CHOICES + k + 1]
                    stt(out=a, in0=y_of[n % 3][k], scalar=w, in1=a, op0=ALU.mult, op1=ALU.add).then_inc(s["summed" if k else "first_added"], 1)
                    if k == 0:
                        dve.wait_ge(s["first_added"], n + 1)

        @block.gpsimd
        def _(pool):
            def inverse_root(dst, var, eps, stats, n, done):
                wait_apart(pool, stats, n)
                nc.gpsimd.tensor_scalar(dst, var, eps, 1.0, ALU.add, ALU.mult).then_inc(s[done + "_sum"], 1)
                pool.wait_ge(s[done + "_sum"], n)
                nc.gpsimd.tensor_tensor(dst, dst, minus_half[:, 0:dst.shape[1]], ALU.pow).then_inc(s[done], 1)

            nc.gpsimd.memset(minus_half[:], -0.5).then_inc(s["ones_set"], 1)
            pool.wait_ge(s["absorb_done"], 3 * XH)
            pool.wait_ge(s["ones_set"], 1)
            nc.gpsimd.memset(z_dec[DDEC:DDEC + 1], 1.0).then_inc(s["ones_set"], 1)
            pool.wait_ge(s["ones_set"], 2)
            for p in range(2):
                nc.gpsimd.memset(a_near[p][:], 0.0)
            nc.gpsimd.memset(hT[:, :, 0:1], 0.0).then_inc(s["ones_set"], 1)
            pool.wait_ge(s["front_in"], 16 * 9)
            pool.wait_ge(s["ones_set"], 3)

            def layer_norm_roots(i, ln):
                mv, rstd = (mv1, rstd1) if ln == "ln1" else (mv23, rstd23)
                for h in range(HALF):
                    inverse_root(rstd[:, h:h + 1], mv[:, h, 1:2], LN_EPS, ln + "_stats", i * HALF + h + 1, ln + "_rstd")

            def mixed(i, f):
                pool.wait_ge(s["mix_used"], i * MIX + f + 1)
                nc.gpsimd.tensor_tensor(mixed_x[f % 2][:], mixed_x[f % 2][:], hT[:, :, 1:T + 1], ALU.add).then_inc(s["mixed_ready"], 1)

            def decay_keys(i, k):
                q = lev[k % 2]
                pool.wait_ge(s["decays_ready"], i * 8 + 2 * k + 2)
                pool.wait_ge(s["k_ready"], i + 1)
                pool.wait_ge(s["r_ready"], i + 1)
                for slot in range(7):
                    half = 1 << (slot or 7)
                    lower = q[:, slot, :].rearrange("p (n two h) -> p n two h", two=2, h=half)[:, :, 0, :]
                    key = kT[:, k, :].rearrange("p (n two h) -> p n two h", two=2, h=half)[:, :, 0, :]
                    nc.gpsimd.tensor_tensor(lower, lower, key, ALU.mult)
                wait_apart(pool, "k_ready", i + 1)
                nc.gpsimd.tensor_scalar(ru[k % 2], rT[:, k, :], bonus[:, k:k + 1], 1.0, ALU.mult, ALU.mult).then_inc(s["k_decayed"], 1)

            def group_roots(i, k):
                v = gmv[:, k % 2, :].rearrange("p (n two) -> p n two", two=2)[:, :, 1]
                inverse_root(grstd[:, k % 2, :], v, GN_EPS, "gn_stats", i * KT + k + 1, "gn_rstd")

            def scatter(i):
                pool.wait_ge(s["ln3_normed"], (i + 1) * HALF)
                wait_apart(pool, "slot_ready", i + 1)
                for h in range(HALF):
                    for k in range(CHOICES):
                        at = bass.IndirectOffsetOnAxis(ap=slot[:, h * CHOICES + k:h * CHOICES + k + 1], axis=0)
                        pool.indirect_dma_start(xs, at, x3[:, h, :], None).then_inc(s["scattered"], 16)

            def batch(i, last_one=None, next_one=None):
                if last_one is not None:
                    layer_norm_roots(last_one, "ln3")
                mixed(i, 0)
                mixed(i, 1)
                if last_one is not None:
                    scatter(last_one)
                for f in range(2, MIX):
                    mixed(i, f)
                decay_keys(i, 0)
                for k in range(KT):
                    if k + 1 < KT:
                        decay_keys(i, k + 1)
                    group_roots(i, k)
                layer_norm_roots(i, "ln2")
                if next_one is not None:
                    layer_norm_roots(next_one, "ln1")

            layer_norm_roots(0, "ln1")
            pool.wait_ge(s["h_ready"], HALF)
            batch(0, None, 1)
            with pool.Fori(1, B - 1) as i:
                batch(i, i - 1, i + 1)
            batch(B - 1, B - 2)
            layer_norm_roots(B - 1, "ln3")
            scatter(B - 1)
            for e in range(E):
                pool.wait_ge(expert_in[e], 32)
                pool.sem_inc(s["expert_ready"], 1)
            for n in range(2):
                pool.wait_ge(s[f"m_y_stored_{n}"], 16 * (STEPS // 2))
            for n in range(NT):
                if n >= 3:
                    pool.wait_ge(s["summed"], n - 2)
                for k in range(CHOICES):
                    at = bass.IndirectOffsetOnAxis(ap=rows[:, n * CHOICES + k:n * CHOICES + k + 1], axis=0)
                    pool.indirect_dma_start(y_of[n % 3][k], None, ys, at).then_inc(s[f"y_in_{n % 3}"], 16)


def _tiles(w, rows=P):
    k, n = w.shape
    return np.ascontiguousarray(w.reshape(k // rows, rows, n).transpose(1, 0, 2).reshape(rows, -1))


def _columns(v):
    v = v.reshape(-1, KT, P)
    return np.ascontiguousarray(v.transpose(2, 0, 1).reshape(P, -1))


def lay_out(n):
    a = {k[8:]: np.asarray(v) for k, v in n.items() if k.startswith("L0_attn_")}
    c = {k[9:]: np.asarray(v) for k, v in n.items() if k.startswith("L0_xattn_")}
    r = constants()
    r["c_iota"] = np.tile(np.arange(E, dtype=np.float32), (P, 1))
    r["c_first"] = np.tile(np.arange(E, dtype=np.float32) * REGION, (P, 1))
    r["c_steps"] = np.tile(np.arange(STEPS + 2, dtype=np.float32), (P, 1))
    r["x"] = np.ascontiguousarray(np.asarray(n["x"]).reshape(B, HALF, P, C).transpose(0, 2, 1, 3))
    ctx = np.asarray(n["ctx_2048"]).transpose(0, 2, 1).reshape(B, KT, P, T)
    r["ctxT"] = np.ascontiguousarray(ctx.transpose(0, 2, 1, 3).reshape(B, P, KT * T))
    r["seg"] = np.ascontiguousarray(np.asarray(n["itok_BxS_0_1023"]).reshape(B, HALF, P).transpose(0, 2, 1))
    r["w1"] = _tiles(a["time_maa_w1"])
    r["w2a"] = np.ascontiguousarray(a["time_maa_w2"][0:4].reshape(4 * DMIX, C))
    r["w2b"] = np.ascontiguousarray(a["time_maa_w2"][4])
    r["maa"] = _columns(np.concatenate([a["time_maa_" + f].reshape(1, C) for f in "xwkvrg"]))
    r["dw1"] = _tiles(a["time_decay_w1"])
    r["dw2"] = np.concatenate([a["time_decay_w2"], a["time_decay"].reshape(1, C)])
    r["bonus"] = _columns(a["time_faaaa"].reshape(1, C))
    r["gam"], r["bet"] = _columns(a["ln_gamma"]), _columns(a["ln_beta"])
    for f in "krvgo":
        r["w" + f] = _tiles(a["W_" + f].T)
    r["wkvc"], r["wdq"] = _tiles(c["W_kvc"]), _tiles(c["W_dq"])
    kr1, kr2 = np.split(c["W_kr"], 2, axis=1)
    r["wkr"] = np.concatenate([kr1, kr2, kr2, kr1, kr2, kr1, kr1, kr2], axis=1)
    r["wqr"] = _tiles(np.tile(c["W_qr"].reshape(QC, XH, 1, ROT), (1, 1, 2, 1)).reshape(QC, -1), QK)
    heads = lambda w: w.reshape(w.shape[0], XH, HD).transpose(2, 1, 0).reshape(HD, -1)
    r["uqT"], r["ukT"], r["uvT"] = (np.ascontiguousarray(heads(c[w])) for w in ("W_uq", "W_uk", "W_uv"))
    r["xo"] = np.ascontiguousarray(c["W_o"].reshape(XH, HD, C).transpose(1, 0, 2).reshape(HD, -1))
    r["router"] = _tiles(np.asarray(n["L0_ffn_router_w"]).T)
    w1 = np.asarray(n["L0_ffn_w1"])
    r["w_gate_up"] = np.ascontiguousarray(
        w1.reshape(E, 2, I, KT, P).transpose(0, 4, 1, 3, 2).reshape(E, P, 2 * KT * I))
    w2 = np.zeros((E, IT * P, C), np.float32)
    w2[:, :I] = np.asarray(n["L0_ffn_w2"]).transpose(0, 2, 1)
    r["w_down"] = np.ascontiguousarray(w2.reshape(E, IT, P, C).transpose(0, 2, 1, 3).reshape(E, P, IT * C))
    return r


def kernel(**inputs):
    import concourse.bacc as bacc
    from concourse.bass_utils import run_bass_kernel_spmd

    arrays = lay_out(inputs)
    nc = bacc.Bacc("TRN2", target_bir_lowering=False, num_devices=1)
    dram = {k: nc.dram_tensor("in_" + k, v.shape, mybir.dt.from_np(v.dtype), kind="ExternalInput").ap()
            for k, v in arrays.items()}
    out = nc.dram_tensor("out_x", (B, T, C), F32, kind="ExternalOutput").ap()
    x2 = nc.dram_tensor("x2_scratch", (B, P, HALF, C), F32, kind="Internal").ap()
    xs = nc.dram_tensor("routed_tokens", (SPARE + P, C), F32, kind="Internal").ap()
    ys = nc.dram_tensor("routed_results", (STEPS * P, C), F32, kind="Internal").ap()
    program(nc, dram, out, x2, xs, ys)
    r = run_bass_kernel_spmd(nc, [{"in_" + k: v for k, v in arrays.items()}], core_ids=[0])
    return r.results[0]["out_x"]
```

```python
from contextlib import ExitStack

import numpy as np
import concourse.bass as bass
from concourse import mybir

F32 = mybir.dt.float32
BF16 = mybir.dt.bfloat16
I32 = mybir.dt.int32
U8 = mybir.dt.uint8
U32 = mybir.dt.uint32
ALU = mybir.AluOpType
ACT = mybir.ActivationFunctionType
AX = mybir.AxisListType

P = 128
B, T, C = 8, 256, 512
KT = C // P
HALF = T // P
RH, HS = 8, 64
MIX, DMIX, DDEC = 5, 32, 64
LN_EPS, GN_EPS = 1e-5, 1e-5 * 8.0 ** 2
LEVELS = 8
XH, HD, ROT = 16, 128, 64
KVC, QC = 128, 192
QK = QC // 2
LOOKBACK, NEG = 8, -1e30
SCALE = 1.0 / np.sqrt(HD + ROT)
E, I, TOP = 8, 352, 8
CHOICES = 2
EARLY = 3
IT = 3
INNER = [(0, 128), (128, 128), (256, 96)]
NT = B * T // P
REGION = B * T + P
SPARE = E * REGION
STEPS = (CHOICES * B * T // P + E - 1 + 1) // 2 * 2
GU_WORDS = 2 * KT * I
E_WORDS = GU_WORDS + IT * C
Y_BUFFERS = 6
DECAY_CAP = 60.0


def constants():
    s, t = np.arange(P)[:, None], np.arange(P)[None, :]
    gap = np.zeros((P, HALF, LEVELS - 1, P), np.float32)
    for level in range(1, LEVELS - 1):
        h = 1 << level
        middle = (t // (2 * h)) * 2 * h + h
        between = np.where(t < middle, (s > t) & (s < middle), (s >= middle) & (s < t))
        gap[:, :, level, :] = -between.astype(np.float32)[:, None, :]
    gap[:, 0, 0, :] = -1.0 * (s > t)
    gap[:, 1, 0, :] = -1.0 * (s < t)
    pick = np.zeros((P, 6, HALF, P), np.int32)
    pick[:, 0] = (s == t)[:, None, :]
    for level in range(5):
        h = 1 << level
        same = (s // (2 * h) == t // (2 * h)) & (s % (2 * h) < h) & (t % (2 * h) >= h)
        pick[:, level + 1] = same[:, None, :]
    half = ROT // 2
    inv = (1.0 / 10000.0 ** (np.arange(half, dtype=np.float32) / half)).astype(np.float32)
    ang = (np.arange(T, dtype=np.float32)[:, None] * inv).astype(np.float32)
    cos, sin = np.cos(ang).T.astype(np.float32), np.sin(ang).T.astype(np.float32)
    q_rot = np.concatenate([cos, cos, sin, sin])
    q_table = np.stack([np.ones((P, T), np.float32), q_rot], 1) * np.float32(SCALE)
    q_table = q_table.reshape(P, 2, HALF, P).transpose(0, 2, 1, 3)
    k_table = np.stack([np.concatenate([cos, cos, cos, -cos]), np.concatenate([-sin, sin, sin, sin])], 1)
    before = np.concatenate([(s < t).astype(np.float32), np.ones((P, P), np.float32)], 1)
    return {
        "c_before": before,
        "c_gap": gap.reshape(P, -1),
        "c_pick": pick.reshape(P, -1),
        "c_ident": np.eye(P, dtype=np.float32),
        "c_keys": np.tile(np.arange(T, dtype=np.float32), (P, 1)),
        "c_qtab": np.ascontiguousarray(q_table.reshape(P, -1)),
        "c_ktab": np.ascontiguousarray(k_table.reshape(P, -1)),
    }


class Arena:

    def __init__(self, tensor, words):
        self.tensor, self.words, self.at = tensor, words, 0

    def take(self, n):
        a = self.tensor[:, self.at:self.at + n]
        self.at += n
        assert self.at <= self.words, self.at
        return a


def program(nc, d, out, x2_dram, xs, ys):
    with ExitStack() as ctx:
        WORDS = 52264
        space = ctx.enter_context(nc.sbuf_tensor("space", [P, WORDS], F32))
        ps = ctx.enter_context(nc.psum_tensor("ps", [P, 8, 512], F32))
        ident_bf = ctx.enter_context(nc.sbuf_tensor("ident_bf", [P, P], BF16))

        minus_half = ctx.enter_context(nc.sbuf_tensor("minus_half", [P, 4], F32))

        def sem(name):
            return ctx.enter_context(nc.semaphore(name))

        ar = Arena(space, WORDS)

        def tiles(n, k):
            return ar.take(n).rearrange("p (k n) -> p k n", k=k)

        gap = tiles(HALF * 7 * P, HALF)
        pick = ar.take(6 * HALF * P // 4).bitcast(U8).rearrange("p (l n) -> p l n", l=6)
        ident = ar.take(P)
        keys = ar.take(T)
        qtab = tiles(HALF * 2 * P, HALF)
        ktab = tiles(2 * T, 2)
        w1 = tiles(KT * MIX * DMIX, KT)
        w2 = tiles(2 * C, 2)
        maa = tiles((MIX + 1) * KT, MIX + 1)
        dw1 = tiles(KT * DDEC, KT)
        dw2 = ar.take(C)
        bonus = ar.take(KT)
        gam = ar.take(KT)
        bet = ar.take(KT)
        projections_at = ar.at
        wr, wk, wv, wg, wo = (tiles(KT * C, KT) for _ in range(5))
        wkvc = tiles(KT * KVC, KT)
        wkr = tiles(2 * P, 2)
        wdq = tiles(KT * QC, KT)
        wqr = tiles(2 * XH * 2 * ROT, 2)
        wqk = tiles(2 * XH * KVC, 2)
        wvo = tiles(XH * C, XH)
        ar.take(ar.at % 2)
        start_of_work = ar.at
        x_in, x1, xn = (tiles(HALF * C, HALF) for _ in range(3))
        xn_at = ar.at - HALF * C
        half_gate = xn
        o_tok = xn
        hT = tiles(KT * (T + 1), KT)
        xx, gT, oT = (tiles(KT * T, KT) for _ in range(3))
        oT_end = ar.at
        xxx = gT
        e_tok = oT.rearrange("p k n -> p (k n)").rearrange("p (k n) -> p k n", k=HALF)
        rT, kT = (tiles(KT * T, KT) for _ in range(2))
        v_tok = tiles(HALF * C, HALF)
        z_a, z_b, z_dec = (ar.take(T) for _ in range(3))
        q_at = ar.at
        lev = [tiles(7 * T, 7) for _ in range(2)]
        mixed_x = [q.rearrange("p l n -> p (l n)")[:, 0:KT * T].rearrange("p (k n) -> p k n", k=KT) for q in lev]
        ru = [ar.take(T) for _ in range(2)]
        a_near = [tiles(HALF * P, HALF) for _ in range(2)]
        a_far = [ar.take(P) for _ in range(2)]
        ctx_at = ar.at
        ctxT = tiles(KT * T, KT)
        kvcT, krT, kr_tmp = (ar.take(T) for _ in range(3))
        kvc = tiles(HALF * KVC, HALF)
        st1, mv1, rstd1 = tiles(HALF * 6, HALF), tiles(HALF * 2, HALF), ar.take(HALF)
        st23, mv23, rstd23 = tiles(HALF * 6, HALF), tiles(HALF * 2, HALF), ar.take(HALF)
        gst, gmv, grstd = tiles(2 * 24, 2), tiles(2 * 8, 2), tiles(2 * 4, 2)
        segi = ar.take(HALF)
        segf, negmax, psumr, prec = ar.take(HALF), ar.take(4), ar.take(4), ar.take(4)
        aq = Arena(space, WORDS)
        aq.at = q_at
        q_lat = aq.take(2 * T).rearrange("p (k n) -> p k n", k=2)
        bias = aq.take(HALF * T // 2).bitcast(BF16).rearrange("p (k n) -> p k n", k=HALF)
        late, early = aq.take(T), aq.take(T)
        q_head = [aq.take(2 * P).rearrange("p (k n) -> p k n", k=2) for _ in range(2)]
        prob = [aq.take(T) for _ in range(3)]
        probT = [aq.take(T).rearrange("p (k n) -> p k n", k=2) for _ in range(2)]
        o_head = [aq.take(P) for _ in range(2)]
        assert aq.at <= q_at + 2 * 7 * T
        x1T = xx
        ap = Arena(space, WORDS)
        ap.at = start_of_work
        uqT = ap.take(XH * QC).rearrange("p (h n) -> p h n", h=XH)
        ukT = ap.take(XH * KVC).rearrange("p (h n) -> p h n", h=XH)
        uvT = ap.take(XH * KVC).rearrange("p (h n) -> p h n", h=XH)
        xo = ap.take(XH * C).rearrange("p (h n) -> p h n", h=XH)

        ap.at = ctx_at
        pick_wide = ap.take(6 * HALF * P).bitcast(I32)

        def small(name, *shape, dt=F32):
            return ctx.enter_context(nc.sbuf_tensor(name, [P, *shape], dt))

        before = small("before", 2, P)
        router = small("router", KT, E)
        iota_e = small("iota_e", E)
        logit = small("logit", HALF, E)
        top, topi, topf = small("top", HALF, TOP), small("topi", HALF, TOP, dt=U32), small("topf", HALF, TOP)
        odds = small("odds", 4, HALF)
        hot = small("hot", HALF, CHOICES, E)
        both = small("both", HALF, E)
        place = small("place", HALF, E)
        picked = small("picked", HALF, CHOICES, E)
        slotf = small("slotf", HALF * CHOICES)
        slot = small("slot", HALF * CHOICES, dt=I32)
        taken = small("taken", E)
        slots = small("slots", NT * CHOICES)
        rows = small("rows", NT * CHOICES, dt=I32)
        experts_of = small("experts_of", NT * CHOICES)
        weights = small("weights", NT * CHOICES)
        n_tiles, n_int, ends = small("n_tiles", E), small("n_int", E, dt=I32), small("ends", 2, E)
        count_int = small("count_int", E, dt=I32)
        steps = small("steps", STEPS + 2)
        step_tab = small("step_tab", 3, STEPS + 2, dt=I32)
        first_row = small("first_row", E)
        counts = small("counts", E)
        x3, x3T = v_tok, rT

        low = Arena(space, projections_at)
        low.at = HALF * 7 * P + 6 * HALF * P // 4
        assert low.take(P).shape == ident.shape
        zeros = low.take(C)
        chosen = low.take(NT * CHOICES * E).rearrange("p (n e) -> p n e", e=E)
        moved = low.take(NT * CHOICES)
        past, past_tiles = (low.take((STEPS + 2) * E).rearrange("p (n e) -> p n e", e=E) for _ in range(2))
        upto = low.take(E * E).rearrange("p (a b) -> p a b", b=E)
        spread = low.take(E * E).rearrange("p (a b) -> p a b", b=E)
        step_e, step_row, step_base = (low.take(STEPS + 2) for _ in range(3))
        am = Arena(space, WORDS)
        am.at = projections_at
        assert EARLY == 3 and 2 * E_WORDS <= 5 * KT * C
        assert xn_at <= projections_at + (E - 1) * E_WORDS and projections_at + E * E_WORDS <= oT_end
        w_experts = am.take(E * E_WORDS)

        def block_of(e):
            n = (e + E - 1) % E
            return w_experts[:, n * E_WORDS:(n + 1) * E_WORDS]

        m_x = [am.take(C) for _ in range(2)]
        m_xT = [am.take(C).rearrange("p (k n) -> p k n", k=KT) for _ in range(2)]
        m_tanh, m_silu, m_h = (am.take(I) for _ in range(3))
        m_hT = [am.take(IT * P).rearrange("p (k n) -> p k n", k=IT) for _ in range(2)]
        m_y = [am.take(C) for _ in range(2)]
        behind = (WORDS - am.at) // (HALF * C)
        low.at = HALF * 7 * P + 6 * HALF * P // 4 + P
        res = [(am if g < behind else low).take(HALF * C).rearrange("p (h n) -> p h n", h=HALF) for g in range(B)]
        ae = Arena(space, WORDS)
        ae.at = projections_at
        y_of = [[ae.take(C) for _ in range(CHOICES)] for _ in range(Y_BUFFERS)]

        s = {n: sem(n) for n in (
            "consts_in", "front_in", "proj_in", "absorb_in_0", "absorb_in_1", "cross_in", "ones_set", "ident_bf_set",
            "absorb_mm", "absorb_done", "x_in_loaded", "ctx_in", "seg_in",
            "ln1_raw", "ln1_stats", "ln1_rstd", "ln1_normed", "h_transposed", "h_ready", "xx_ready", "xxx_ready",
            "z_mm", "z_ready", "mix_mm", "mix_used", "mixed_ready", "zdec_mm", "zdec_ready", "k_mm", "k_ready",
            "dd_mm", "dd_capped", "e_ready", "v_mm", "v_ready", "r_mm", "r_ready", "g_mm", "g_tanh", "g_ready",
            "gap_mm", "decays_ready", "k_decayed", "r_decayed", "gram_far", "gram_near", "far_copied", "near_picked",
            "av_done", "gn_raw", "gn_stats", "gn_rstd", "o_normed", "o_transposed", "o_affine", "o_gated",
            "wo_mm", "x1_ready",
            "kvc_mm", "kvc_ready", "kr_mm", "kr_cos", "kr_sin", "kr_ready",
            "seg_float", "late_set", "early_set", "bad_set", "bias_ready",
            "ln2_raw", "ln2_stats", "ln2_rstd", "ln2_normed", "x1_transposed", "x1T_ready", "qlat_mm", "qlat_ready",
            "head_mm", "head_ready", "score_mm", "max_ready", "exp_done", "sum_inverted", "prob_ready",
            "prob_transposed", "probT_ready", "pv_mm", "o_head_ready", "out_mm", "x2_ready", "x2_stored",
            "router_in", "route_link", "ln3_raw", "ln3_stats", "ln3_rstd", "ln3_normed", "x3_transposed", "x3T_ready",
            "logit_mm", "topi_ready", "gap12", "odds_ready", 
            "w_kept", "both_ready", "rank_mm", "taken_moved", 
            "slot_ready", "slots_kept", "scattered", "table_link", "table_ready", "padded",
            "expert_in", "late_expert_in", "expert_ready", "zeros_set", "counted", "rows_ready", "gate_mm", "up_mm", "m_x_in_0", "m_x_in_1", "m_x_transposed", "m_xT_ready", "m_tanhed", "m_silued",
            "m_h_ready", "m_h_transposed", "m_hT_ready", "down_mm", "m_y_ready", "m_y_stored_0", "m_y_stored_1",
            "res_in", "first_added", "summed", "stored",
            "waited_apart",
            "ln1_rstd_sum", "ln2_rstd_sum", "ln3_rstd_sum", "gn_rstd_sum", "level_picked",
        )}

        y_in = [sem(f"y_in_{n}") for n in range(Y_BUFFERS)]

        def after(eng, signal, n):
            if not isinstance(n, int) or n > 0:
                eng.wait_ge(s[signal], n)

        def wait_apart(eng, signal, n):
            eng.wait_ge(s[signal], n)
            eng.sem_inc(s["waited_apart"], 1)

        block = ctx.enter_context(nc.Block())

        @block.sync
        def _(sp):
            def load(dst, name, signal):
                sp.dma_start(dst, d[name]).then_inc(s[signal], 16)

            flat = "p k n -> p (k n)"
            load(ident, "c_ident", "consts_in")
            for part in range(2):
                heads = slice(part * XH // 2, (part + 1) * XH // 2)
                for factor, name in ((uqT, "uqT"), (ukT, "ukT"), (uvT, "uvT"), (xo, "xo")):
                    sp.dma_start(factor[:, heads, :], d[name].rearrange("p (h n) -> p h n", h=XH)[:, heads, :]
                                 ).then_inc(s[f"absorb_in_{part}"], 16)
            load(pick_wide, "c_pick", "consts_in")
            load(w1.rearrange(flat), "w1", "front_in")
            load(w2[:, 0, :], "w2a", "front_in")
            load(w2[0:DMIX, 1, :], "w2b", "front_in")
            load(maa.rearrange(flat), "maa", "front_in")
            load(dw1.rearrange(flat), "dw1", "front_in")
            load(dw2[0:DDEC + 1], "dw2", "front_in")
            load(bonus, "bonus", "front_in")
            load(gam, "gam", "front_in")
            load(bet, "bet", "front_in")
            load(before[:].rearrange("p a n -> p (a n)"), "c_before", "router_in")
            load(router[:].rearrange("p k e -> p (k e)"), "router", "router_in")
            load(iota_e[:], "c_iota", "router_in")
            load(taken[:], "c_first", "router_in")
            load(first_row[:], "c_first", "router_in")
            load(steps[:], "c_steps", "router_in")

            def loads(i):
                after(sp, "x1_ready", i * HALF)
                sp.dma_start(x_in[:], d["x"][i]).then_inc(s["x_in_loaded"], 16)
                after(sp, "qlat_mm", i)
                sp.dma_start(ctxT.rearrange(flat), d["ctxT"][i]).then_inc(s["ctx_in"], 16)
                after(sp, "seg_float", i)
                sp.dma_start(segi.bitcast(I32), d["seg"][i]).then_inc(s["seg_in"], 16)

            def store(i):
                sp.wait_ge(s["x2_ready"], (i + 1) * HALF)
                sp.dma_start(x2_dram[i], x1[:]).then_inc(s["x2_stored"], 16)

            load(wk.rearrange(flat), "wk", "proj_in")
            load(wv.rearrange(flat), "wv", "proj_in")
            sp.wait_ge(s["absorb_done"], 3 * XH)
            sp.wait_ge(s["ident_bf_set"], 2)
            loads(0)
            for w, n in ((wr, "wr"), (wg, "wg")):
                load(w.rearrange(flat), n, "proj_in")
            load(gap.rearrange(flat), "c_gap", "proj_in")
            load(wo.rearrange(flat), "wo", "proj_in")
            load(wkvc.rearrange(flat), "wkvc", "cross_in")
            load(wkr.rearrange(flat), "wkr", "cross_in")
            load(wdq.rearrange(flat), "wdq", "cross_in")
            sp.dma_start(wqr[0:QK], d["wqr"].rearrange("p (k n) -> p k n", k=2)).then_inc(s["cross_in"], 16)
            load(keys, "c_keys", "cross_in")
            load(qtab.rearrange(flat), "c_qtab", "cross_in")
            load(ktab.rearrange(flat), "c_ktab", "cross_in")
            loads(1)
            store(0)
            with sp.Fori(1, B - 1) as i:
                loads(i + 1)
                store(i)
            sp.wait_ge(s["wo_mm"], B * HALF)
            sp.wait_ge(s["qlat_mm"], B)
            for e in range(EARLY):
                sp.dma_start(block_of(e), d["w_experts"][e]).then_inc(s["expert_in"], 16)
            store(B - 1)

            sp.wait_ge(s["zeros_set"], 1)
            sp.wait_ge(s["counted"], 1)
            for n in range(E):
                first = sp.value_load(count_int[0:1, n:n + 1], min_val=0, max_val=B * T)
                sp.dma_start(xs[bass.ds(first + n * REGION, P), :], zeros).then_inc(s["padded"], 16)
            sp.dma_start(xs[SPARE:SPARE + P, :], zeros).then_inc(s["padded"], 16)
            sp.wait_ge(s["x2_stored"], 16 * B)
            sp.wait_ge(s["scattered"], 16 * B * HALF * CHOICES)
            sp.wait_ge(s["table_ready"], 1)
            sp.wait_ge(s["padded"], 16 * (E + 1))
            for n in range(2):
                row = sp.value_load(step_tab[0:1, 1, n:n + 1], min_val=0, max_val=SPARE)
                sp.dma_start(m_x[n], xs[bass.ds(row, P), :]).then_inc(s[f"m_x_in_{n}"], 16)
            with sp.Fori(0, STEPS // 2) as pair:
                for n in range(2):
                    j = pair * 2 + n
                    row = sp.value_load(step_tab[0:1, 1, bass.ds(j + 2, 1)], min_val=0, max_val=SPARE)
                    sp.wait_ge(s["m_x_transposed"], j + 1)
                    sp.dma_start(m_x[n], xs[bass.ds(row, P), :]).then_inc(s[f"m_x_in_{n}"], 16)
                    sp.wait_ge(s["m_y_ready"], j + 1)
                    sp.dma_start(ys[bass.ds(j * P, P), :], m_y[n]).then_inc(s[f"m_y_stored_{n}"], 16)
            for n in range(2):
                sp.wait_ge(s[f"m_x_in_{n}"], 16 * (STEPS // 2 + 1))
            sp.wait_ge(s["stored"], 16 * NT)

        @block.tensor
        def _(pe):
            mm = nc.tensor.matmul

            def accumulate(dst, pairs):
                for n, (a, b) in enumerate(pairs):
                    last = mm(dst, a, b, start=(n == 0), stop=(n == len(pairs) - 1))
                return last

            for h in range(XH):
                if h % (XH // 2) == 0:
                    pe.wait_ge(s[f"absorb_in_{h // (XH // 2)}"], 16 * 4)
                if h >= 2:
                    pe.wait_ge(s["absorb_done"], 3 * (h - 1))
                b = 4 * (h % 2)
                mm(ps[0:QK, b, 0:KVC], uqT[:, h, 0:QK], ukT[:, h, :], start=True, stop=True)
                mm(ps[0:QK, b, KVC:2 * KVC], uqT[:, h, QK:QC], ukT[:, h, :], start=True, stop=True)
                mm(ps[:, b + 1, :], uvT[:, h, :], xo[:, h, :], start=True, stop=True).then_inc(s["absorb_mm"], 1)
            pe.wait_ge(s["absorb_done"], 3 * XH)
            pe.wait_ge(s["consts_in"], 32)
            pe.wait_ge(s["front_in"], 16 * 9)
            pe.wait_ge(s["ones_set"], 3)
            pe.wait_ge(s["ident_bf_set"], 2)

            def latent_columns(i):
                pe.wait_ge(s["ctx_in"], (i + 1) * 16)
                pe.wait_ge(s["o_normed"], i * KT + 3)
                accumulate(ps[:, 6, 0:T], [(wkvc[:, k, :], ctxT[:, k, :]) for k in range(KT)])

            def latent_rows(i):
                for h in range(HALF):
                    last = accumulate(ps[:, 6, T + h * P:T + (h + 1) * P],
                                      [(ctxT[:, k, h * P:(h + 1) * P], wkvc[:, k, :]) for k in range(KT)])
                last.then_inc(s["kvc_mm"], 1)

            def rotary_keys(i):
                pe.wait_ge(s["kvc_ready"], i + 1)
                pe.wait_ge(s["o_normed"], (i + 1) * KT)
                mm(ps[:, 7, 0:T], wkr[:, 0, :], kvcT, start=True, stop=True)
                mm(ps[:, 7, T:2 * T], wkr[:, 1, :], kvcT, start=True, stop=True).then_inc(s["kr_mm"], 1)

            def transposes(i, normed, src, b0, signal):
                for h in range(HALF):
                    pe.wait_ge(s[normed], i * HALF + h + 1)
                    for k in range(KT):
                        last = nc.tensor.transpose(ps[:, b0 + h, k * P:(k + 1) * P], src[:, h, k * P:(k + 1) * P], ident)
                    last.then_inc(s[signal], 1)

            pair_of = [ps[:, 2 * n:2 * n + 2, :].rearrange("p a (k n) -> p (a k) n", n=T) for n in range(4)]

            def low_rank(i):
                pe.wait_ge(s["xxx_ready"], i + 1)
                accumulate(ps[:, 4, 0:T], [(w1[:, k, 0:P], xxx[:, k, :]) for k in range(KT)])
                accumulate(ps[0:DMIX, 4, T:2 * T], [(w1[:, k, P:P + DMIX], xxx[:, k, :]) for k in range(KT)]).then_inc(s["z_mm"], 1)

            def mix(i, f):
                if f >= 2:
                    after(pe, "mix_used", i * MIX + f - 1)
                dst = pair_of[f % 2]
                for k in range(KT):
                    if f < 4:
                        rows = slice(DMIX * f, DMIX * (f + 1))
                        last = mm(dst[:, k, :], w2[rows, 0, k * P:(k + 1) * P], z_a[rows], start=True, stop=True, tile_position=(DMIX * f, 0))
                    else:
                        last = mm(dst[:, k, :], w2[0:DMIX, 1, k * P:(k + 1) * P], z_b[0:DMIX], start=True, stop=True)
                last.then_inc(s["mix_mm"], 1)

            def project(i, f, w, x, b, signal, tiles=range(KT)):
                pe.wait_ge(s["mixed_ready"], i * MIX + f + 1)
                for k in tiles:
                    last = accumulate(pair_of[b][:, k, :], [(w[:, c, k * P:(k + 1) * P], x[:, c, :]) for c in range(KT)])
                if k == KT - 1:
                    last.then_inc(s[signal], 1)

            def time_mix(i, last_one):
                pe.wait_ge(s["z_ready"], i + 1)
                mix(i, 0)
                mix(i, 1)
                mix(i, 2)
                pe.wait_ge(s["mixed_ready"], i * MIX + 1)
                accumulate(ps[0:DDEC, 4, 0:T], [(dw1[:, k, :], mixed_x[0][:, k, :]) for k in range(KT)]).then_inc(s["zdec_mm"], 1)
                if last_one is None:
                    pe.wait_ge(s["proj_in"], 16 * 6)
                after(pe, "x2_ready", i * HALF)
                project(i, 1, wk, mixed_x[1], 3, "k_mm")
                if last_one is not None:
                    route_ranks(last_one)
                mix(i, 3)
                pe.wait_ge(s["mixed_ready"], i * MIX + 3)
                pe.wait_ge(s["k_ready"], i + 1)
                for h in range(HALF):
                    last = accumulate(ps[:, 6 + h, :], [(mixed_x[0][:, k, h * P:(h + 1) * P], wv[:, k, :]) for k in range(KT)])
                last.then_inc(s["v_mm"], 1)
                pe.wait_ge(s["zdec_ready"], i + 1)
                after(pe, "taken_moved", i)
                for h in range(HALF):
                    last = mm(ps[:, 4 + h, :], z_dec[0:DDEC + 1, h * P:(h + 1) * P], dw2[0:DDEC + 1], start=True, stop=True)
                last.then_inc(s["dd_mm"], 1)
                mix(i, 4)
                pe.wait_ge(s["dd_capped"], i + 1)
                project(i, 3, wr, mixed_x[1], 2, "r_mm")
                gaps(i, 0, [0])
                pe.wait_ge(s["v_ready"], i + 1)
                project(i, 4, wg, mixed_x[0], 3, "g_mm", range(KT // 2))
                gaps(i, 0, [1])
                project(i, 4, wg, mixed_x[0], 3, "g_mm", range(KT // 2, KT))

            def gaps(i, k, halves=range(HALF)):
                for h in halves:
                    if k == 0 and h == 0:
                        pe.wait_ge(s["e_ready"], i + 1)
                        pe.wait_ge(s["mix_used"], (i + 1) * MIX)
                    after(pe, "decays_ready", i * 8 + 2 * k + h)
                    w = e_tok[:, h, k * P:(k + 1) * P]
                    mm(ps[:, 0, :], w, gap[:, h, 0:4 * P], start=True, stop=True)
                    mm(ps[:, 1, 0:3 * P], w, gap[:, h, 4 * P:7 * P], start=True, stop=True).then_inc(s["gap_mm"], 1)

            def grams(i, h):
                k, p = divmod(h, 2)
                rows = slice(HS * p, HS * (p + 1))
                at = (HS * p, 0)
                q = lev[(k + 1) % 2]
                if p == 0:
                    pe.wait_ge(s["k_decayed"], i * KT + k + 1)
                    pe.wait_ge(s["r_decayed"], i * KT + k + 1)
                after(pe, "far_copied", i * RH + h)
                for t in range(HALF):
                    o = t * P
                    mm(ps[:, 5, o:o + P], q[rows, 5, o:o + P], q[rows, 5, o:o + P], start=True, stop=True, tile_position=at)
                    mm(ps[0:64, 5, T + 64 * t:T + 64 * t + 64], q[rows, 6, o:o + 64], q[rows, 6, o + 64:o + P],
                       start=True, stop=True, tile_position=at)
                mm(ps[:, 5, 3 * P:4 * P], q[rows, 0, 0:P], q[rows, 0, P:T], start=True, stop=True, tile_position=at).then_inc(s["gram_far"], 1)
                for b in range(3):
                    after(pe, "near_picked", i * (3 * RH) + (3 * h + b - 2 if h else 0))
                    for t in range(HALF):
                        o = slice(t * P, (t + 1) * P)
                        for n in range(2):
                            level = 2 * b + n - 1
                            left, right = ((kT[rows, k, o], ru[k % 2][rows, o]), (kT[rows, k, o], rT[rows, k, o]))[n] if b == 0 else (
                                q[rows, level, o], q[rows, level, o])
                            last = mm(ps[:, 2 + b, n * T + t * P:n * T + (t + 1) * P], left, right,
                                      start=True, stop=True, tile_position=at)
                    last.then_inc(s["gram_near"], 1)

            def values(i, h):
                k, p = divmod(h, 2)
                b = 6 + k % 2
                if h == 0:
                    pe.wait_ge(s["g_ready"], i + 1)
                if k >= 2 and p == 0:
                    after(pe, "o_normed", i * KT + k - 1)
                pe.wait_ge(s["near_picked"], i * (3 * RH) + 3 * (h + 1))
                v = [v_tok[:, t, h * HS:(h + 1) * HS] for t in range(HALF)]
                dst = [ps[:, b, t * P + p * HS:t * P + (p + 1) * HS] for t in range(HALF)]
                mm(dst[0], a_near[p][:, 0, :], v[0], start=True, stop=True)
                accumulate(dst[1], [(a_near[p][:, 1, :], v[1]), (a_far[p], v[0])]).then_inc(s["av_done"], 1)

            def output(i, last_one):
                if last_one is None:
                    pe.wait_ge(s["cross_in"], 16 * 7)
                latent_columns(i)
                pe.wait_ge(s["decays_ready"], (i + 1) * 8)
                for k in range(KT):
                    pe.wait_ge(s["o_normed"], i * KT + k + 1)
                    for t in range(HALF):
                        c = (k % 2) * T + t * P
                        last = nc.tensor.transpose(ps[:, k // 2, c:c + P], o_tok[:, t, k * P:(k + 1) * P], ident)
                    last.then_inc(s["o_transposed"], 1)
                latent_rows(i)
                pe.wait_ge(s["o_gated"], i + 1)
                for t in range(HALF):
                    accumulate(ps[:, 2 + t, :], [(oT[:, k, t * P:(t + 1) * P], wo[:, k, :]) for k in range(KT)]).then_inc(s["wo_mm"], 1)

            def query_latent(i):
                pe.wait_ge(s["x1T_ready"], (i + 1) * HALF)
                for a in range(2):
                    last = accumulate(ps[0:QK, 6, a * T:(a + 1) * T], [(wdq[:, k, a * QK:(a + 1) * QK], x1T[:, k, :]) for k in range(KT)])
                last.then_inc(s["qlat_mm"], 1)
                pe.wait_ge(s["qlat_ready"], i + 1)
                pe.wait_ge(s["kr_ready"], i + 1)
                pe.wait_ge(s["bias_ready"], (i + 1) * HALF)

            UNITS = HALF * XH

            def head_query(i, u):
                t, h = divmod(u, XH)
                if u >= 2:
                    after(pe, "head_ready", i * UNITS + u - 1)
                q = q_lat[0:QK, :, t * P:(t + 1) * P]
                accumulate(ps[:, u % 2, 0:P], [(wqk[0:QK, a, h * KVC:(h + 1) * KVC], q[:, a, :]) for a in range(2)])
                for a in range(2):
                    last = mm(ps[:, u % 2, P:2 * P], wqr[0:QK, a, h * P:(h + 1) * P], q[:, a, :], start=(a == 0), stop=(a == 1))
                last.then_inc(s["head_mm"], 1)

            def scores(i, u):
                t = u // XH
                pe.wait_ge(s["head_ready"], i * UNITS + u + 1)
                if u >= 2:
                    after(pe, "exp_done", i * UNITS + u - 1)
                q, dst = q_head[u % 2], ps[:, 2 + u % 2, 0:T]
                mm(dst, q[:, 0, :], kvcT, start=True, stop=False)
                mm(dst, q[:, 1, :], krT, start=False, stop=False)
                mm(dst, ident_bf[:], bias[:, t, :], start=False, stop=True).then_inc(s["score_mm"], 1)

            def prob_transpose(i, u):
                pe.wait_ge(s["prob_ready"], i * UNITS + u + 1)
                if u >= 2:
                    after(pe, "probT_ready", i * UNITS + u - 1)
                for a in range(2):
                    last = nc.tensor.transpose(ps[:, 4 + u % 2, a * P:(a + 1) * P], prob[u % 3][:, a * P:(a + 1) * P], ident)
                last.then_inc(s["prob_transposed"], 1)

            def weigh(i, u):
                pe.wait_ge(s["probT_ready"], i * UNITS + u + 1)
                if u >= 1:
                    after(pe, "o_head_ready", i * UNITS + u)
                accumulate(ps[:, 6, 0:P], [(kvc[:, a, :], probT[u % 2][:, a, :]) for a in range(2)]).then_inc(s["pv_mm"], 1)

            def head_output(i, u):
                t, h = divmod(u, XH)
                pe.wait_ge(s["o_head_ready"], i * UNITS + u + 1)
                if h == 0:
                    after(pe, "x2_ready", i * HALF + t)
                mm(ps[:, 7, :], o_head[u % 2], wvo[:, h, :], start=(h == 0), stop=(h == XH - 1)).then_inc(s["out_mm"], 1)

            def route_logits(i):
                transposes(i, "ln3_normed", x3, 0, "x3_transposed")
                for h in range(HALF):
                    pe.wait_ge(s["x3T_ready"], i * HALF + h + 1)
                    last = accumulate(ps[:, 5, h * E:(h + 1) * E], [(x3T[:, k, h * P:(h + 1) * P], router[:, k, :]) for k in range(KT)])
                last.then_inc(s["logit_mm"], 1)

            def route_ranks(i):
                pe.wait_ge(s["both_ready"], i + 1)
                b = both[:].rearrange("p h e -> p (h e)")
                mm(ps[:, 5, HALF * E:2 * HALF * E], before[:, 0, :], b, start=True, stop=True)
                mm(ps[:, 5, 2 * HALF * E:3 * HALF * E], before[:, 1, :], b, start=True, stop=True).then_inc(s["rank_mm"], 1)

            def batch(i, last_one=None):
                transposes(i, "ln1_normed", xn, 2, "h_transposed")
                if last_one is not None:
                    route_logits(last_one)
                low_rank(i)
                time_mix(i, last_one)
                for h in range(RH):
                    if h // 2 + 1 < KT:
                        gaps(i, h // 2 + 1, [h % 2])
                    grams(i, h)
                    if h >= 1:
                        values(i, h - 1)
                values(i, RH - 1)
                output(i, last_one)
                rotary_keys(i)
                transposes(i, "ln2_normed", xn, 4, "x1_transposed")
                query_latent(i)
                head_query(i, 0)
                for u in range(UNITS + 2):
                    if u < UNITS:
                        scores(i, u)
                    if 1 <= u <= UNITS:
                        prob_transpose(i, u - 1)
                    if u + 1 < UNITS:
                        head_query(i, u + 1)
                    if 1 <= u <= UNITS:
                        weigh(i, u - 1)
                    if u >= 2:
                        head_output(i, u - 2)

            pe.wait_ge(s["router_in"], 16 * 6)
            batch(0)
            with pe.Fori(1, B) as i:
                batch(i, i - 1)
            pe.wait_ge(s["x2_ready"], B * HALF)
            route_logits(B - 1)
            route_ranks(B - 1)

            pe.wait_ge(s["table_ready"], 1)

            def take_tokens(j, n):
                pe.wait_ge(s[f"m_x_in_{n}"], (j - n) * 8 + 16)
                after(pe, "m_xT_ready", j)
                for k in range(KT):
                    last = nc.tensor.transpose(ps[:, 2 + n, k * P:(k + 1) * P], m_x[n][:, k * P:(k + 1) * P], ident)
                last.then_inc(s["m_x_transposed"], 1)

            def gate_up(j, n):
                e = pe.value_load(step_tab[0:1, 0, bass.ds(j, 1)], min_val=0, max_val=E - 1)
                ready = pe.value_load(step_tab[0:1, 2, bass.ds(j, 1)], min_val=1, max_val=E)
                pe.wait_ge(s["expert_ready"], ready)
                pe.wait_ge(s["m_xT_ready"], j + 1)
                after(pe, "m_h_ready", j)
                for a in range(2):
                    last = accumulate(ps[:, a, 0:I], [(m_xT[n][:, k, :], w_experts[:, bass.ds(e * E_WORDS + (a * KT + k) * I, I)])
                                                      for k in range(KT)])
                    last.then_inc(s["gate_mm" if a == 0 else "up_mm"], 1)

            def turn_inner(j):
                pe.wait_ge(s["m_h_ready"], j + 1)
                after(pe, "m_hT_ready", j)
                for a, (o, m) in enumerate(INNER):
                    last = nc.tensor.transpose(ps[0:m, 4, a * P:(a + 1) * P], m_h[:, o:o + m], ident)
                last.then_inc(s["m_h_transposed"], 1)

            def down(j, n):
                e = pe.value_load(step_tab[0:1, 0, bass.ds(j, 1)], min_val=0, max_val=E - 1)
                pe.wait_ge(s["m_hT_ready"], j + 1)
                if n == 1 or not isinstance(j, int):
                    after(pe, "m_y_ready", j - 1)
                accumulate(ps[:, 5 + n, :], [(m_hT[n][0:m, a, :], w_experts[0:m, bass.ds(e * E_WORDS + GU_WORDS + a * C, C)])
                                             for a, (o, m) in enumerate(INNER)]).then_inc(s["down_mm"], 1)

            take_tokens(0, 0)
            gate_up(0, 0)
            take_tokens(1, 1)
            turn_inner(0)
            gate_up(1, 1)
            take_tokens(2, 0)
            down(0, 0)
            turn_inner(1)
            with pe.Fori(1, STEPS // 2) as pair:
                for n in range(2):
                    j = pair * 2 + n
                    gate_up(j, n)
                    take_tokens(j + 1, 1 - n)
                    down(j - 1, 1 - n)
                    turn_inner(j)
            down(STEPS - 1, 1)

        @block.scalar
        def _(act):
            fn = nc.scalar.activation

            for h in range(XH):
                act.wait_ge(s["absorb_mm"], h + 1)
                b = 4 * (h % 2)
                for a in range(2):
                    nc.scalar.copy(wqk[0:QK, a, h * KVC:(h + 1) * KVC], ps[0:QK, b, a * KVC:(a + 1) * KVC]).then_inc(s["absorb_done"], 1)
                nc.scalar.copy(wvo[:, h, :], ps[:, b + 1, :]).then_inc(s["absorb_done"], 1)

            def latents(i):
                act.wait_ge(s["kvc_mm"], i + 1)
                nc.scalar.copy(kvcT, ps[:, 6, 0:T])
                nc.scalar.copy(kvc.rearrange("p k n -> p (k n)"), ps[:, 6, T:2 * T]).then_inc(s["kvc_ready"], 1)

            def take_transposed(i, signal_in, dst, b0, signal):
                for h in range(HALF):
                    act.wait_ge(s[signal_in], i * HALF + h + 1)
                    nc.scalar.copy(dst[:, :, h * P:(h + 1) * P], ps[:, b0 + h, :].rearrange("p (k n) -> p k n", k=KT)).then_inc(s[signal], 1)

            def pair_of(n):
                return ps[:, 2 * n:2 * n + 2, :].rearrange("p a (k n) -> p (a k) n", n=T)

            def squash_low_rank(i):
                act.wait_ge(s["z_mm"], i + 1)
                fn(z_a, ps[:, 4, 0:T], ACT.Tanh)
                fn(z_b[0:DMIX], ps[0:DMIX, 4, T:2 * T], ACT.Tanh).then_inc(s["z_ready"], 1)

            def time_mix(i, last_one):
                act.wait_ge(s["zdec_mm"], i + 1)
                fn(z_dec[0:DDEC], ps[0:DDEC, 4, 0:T], ACT.Tanh).then_inc(s["zdec_ready"], 1)
                if last_one is not None:
                    route_odds(last_one)
                act.wait_ge(s["k_mm"], i + 1)
                nc.scalar.copy(kT[:], pair_of(3)).then_inc(s["k_ready"], 1)
                act.wait_ge(s["dd_capped"], i + 1)
                fn(e_tok[:], e_tok[:], ACT.Exp).then_inc(s["e_ready"], 1)
                act.wait_ge(s["v_mm"], i + 1)
                after(act, "scattered", i * (16 * HALF * CHOICES))
                nc.scalar.copy(v_tok[:], ps[:, 6:8, :]).then_inc(s["v_ready"], 1)
                act.wait_ge(s["r_mm"], i + 1)
                nc.scalar.copy(rT[:], pair_of(2)).then_inc(s["r_ready"], 1)
                decays(i, 0)
                act.wait_ge(s["g_mm"], i + 1)
                fn(half_gate.rearrange("p h (k n) -> p (h k) n", n=T), pair_of(3), ACT.Tanh, scale=0.5).then_inc(s["g_tanh"], 1)

            def decays(i, k, halves=range(HALF)):
                q = lev[(k + 1) % 2]
                if k >= 2:
                    after(act, "gram_near", i * (3 * RH) + 6 * (k - 1))
                for h in halves:
                    act.wait_ge(s["gap_mm"], i * 8 + 2 * k + h + 1)
                    o = slice(h * P, (h + 1) * P)
                    fn(q[:, 0:4, o], ps[:, 0, :].rearrange("p (l n) -> p l n", l=4), ACT.Exp)
                    fn(q[:, 4:7, o], ps[:, 1, 0:3 * P].rearrange("p (l n) -> p l n", l=3), ACT.Exp).then_inc(s["decays_ready"], 1)

            def far(i, h):
                p = h % 2
                act.wait_ge(s["gram_far"], i * RH + h + 1)
                if h >= 2:
                    after(act, "av_done", i * RH + h - 1)
                near = ps[:, 5, 0:T].rearrange("p (t n) -> p t n", t=HALF)
                nc.scalar.copy(a_near[p][0:32, :, 32:64], near[0:32, :, 32:64])
                nc.scalar.copy(a_near[p][64:96, :, 96:128], near[64:96, :, 96:128])
                nc.scalar.copy(a_near[p][0:64, :, 64:128], ps[0:64, 5, T:T + P].rearrange("p (t n) -> p t n", t=HALF))
                nc.scalar.copy(a_far[p], ps[:, 5, 3 * P:4 * P]).then_inc(s["far_copied"], 1)

            def affine(i):
                for k in range(KT):
                    after(act, "o_transposed", i * KT + (k // 2 + 1) * 2)
                    c = (k % 2) * T
                    fn(oT[:, k, :], ps[:, k // 2, c:c + T], ACT.Identity, scale=gam[:, k:k + 1], bias=bet[:, k:k + 1]).then_inc(s["o_affine"], 1)

            def query_latent(i):
                act.wait_ge(s["qlat_mm"], i + 1)
                nc.scalar.copy(q_lat[0:QK], ps[0:QK, 6, :].rearrange("p (a n) -> p a n", a=2)).then_inc(s["qlat_ready"], 1)

            UNITS = HALF * XH

            def exponentials(i, u):
                act.wait_ge(s["max_ready"], i * UNITS + u + 1)
                if u >= 3:
                    after(act, "prob_transposed", i * UNITS + u - 2)
                if u >= 4:
                    after(act, "sum_inverted", i * UNITS + u - 3)
                fn(prob[u % 3], ps[:, 2 + u % 2, 0:T], ACT.Exp, bias=negmax[:, u % 4:u % 4 + 1],
                   accum_out=psumr[:, u % 4:u % 4 + 1]).then_inc(s["exp_done"], 1)

            def prob_back(i, u):
                act.wait_ge(s["prob_transposed"], i * UNITS + u + 1)
                if u >= 2:
                    after(act, "pv_mm", i * UNITS + u - 1)
                nc.scalar.copy(probT[u % 2][:], ps[:, 4 + u % 2, 0:T].rearrange("p (a n) -> p a n", a=2)).then_inc(s["probT_ready"], 1)

            def o_back(i, u):
                act.wait_ge(s["pv_mm"], i * UNITS + u + 1)
                if u >= 2:
                    after(act, "out_mm", i * UNITS + u - 1)
                nc.scalar.copy(o_head[u % 2], ps[:, 6, 0:P]).then_inc(s["o_head_ready"], 1)

            def route(i):
                for h in range(HALF):
                    act.wait_ge(s["x3_transposed"], i * HALF + h + 1)
                    nc.scalar.copy(x3T[:, :, h * P:(h + 1) * P], ps[:, h, :].rearrange("p (k n) -> p k n", k=KT)).then_inc(s["x3T_ready"], 1)

            def route_odds(i):
                act.wait_ge(s["gap12"], i + 1)
                fn(odds[:, 1, :], odds[:, 0, :], ACT.Exp).then_inc(s["odds_ready"], 1)

            def batch(i, last_one=None):
                take_transposed(i, "h_transposed", hT[:, :, 1:T + 1], 2, "h_ready")
                if last_one is not None:
                    route(last_one)
                squash_low_rank(i)
                time_mix(i, last_one)
                for h in range(RH):
                    if h // 2 + 1 < KT:
                        decays(i, h // 2 + 1, [h % 2])
                    far(i, h)
                affine(i)
                latents(i)
                take_transposed(i, "x1_transposed", x1T, 4, "x1T_ready")
                query_latent(i)
                for u in range(UNITS + 1):
                    if u >= 1:
                        prob_back(i, u - 1)
                    if u < UNITS:
                        exponentials(i, u)
                    if u >= 1:
                        o_back(i, u - 1)

            act.wait_ge(s["front_in"], 16 * 9)
            act.wait_ge(s["ones_set"], 3)
            batch(0)
            with act.Fori(1, B) as i:
                batch(i, i - 1)
            route(B - 1)
            route_odds(B - 1)

            def take_tokens(j, n):
                act.wait_ge(s["m_x_transposed"], j + 1)
                if n == 1 or not isinstance(j, int):
                    after(act, "gate_mm", j - 1)
                    after(act, "up_mm", j - 1)
                nc.scalar.copy(m_xT[n][:], ps[:, 2 + n, :].rearrange("p (k n) -> p k n", k=KT)).then_inc(s["m_xT_ready"], 1)

            def squash(j):
                act.wait_ge(s["gate_mm"], j + 1)
                after(act, "m_silued", j)
                fn(m_tanh, ps[:, 0, 0:I], ACT.Tanh, scale=0.5).then_inc(s["m_tanhed"], 1)

            def turn_inner(j, n):
                act.wait_ge(s["m_h_transposed"], j + 1)
                if n == 1 or not isinstance(j, int):
                    after(act, "down_mm", j - 1)
                nc.scalar.copy(m_hT[n][:, 0:2, :], ps[:, 4, 0:2 * P].rearrange("p (k n) -> p k n", k=2))
                nc.scalar.copy(m_hT[n][0:INNER[2][1], 2, :], ps[0:INNER[2][1], 4, 2 * P:3 * P]).then_inc(s["m_hT_ready"], 1)

            take_tokens(0, 0)
            squash(0)
            take_tokens(1, 1)
            turn_inner(0, 0)
            squash(1)
            take_tokens(2, 0)
            turn_inner(1, 1)
            with act.Fori(1, STEPS // 2) as pair:
                for n in range(2):
                    j = pair * 2 + n
                    squash(j)
                    take_tokens(j + 1, 1 - n)
                    turn_inner(j, n)
            for n in range(NT):
                act.wait_ge(s["summed"], n + 1)
                act.dma_start(out[n // HALF, (n % HALF) * P:(n % HALF + 1) * P, :], res[n // HALF][:, n % HALF, :]).then_inc(s["stored"], 16)

        @block.vector
        def _(dve):
            ts, tt, stt = nc.vector.tensor_scalar, nc.vector.tensor_tensor, nc.vector.scalar_tensor_tensor

            def norm_stats(i, ln, src, halves=range(HALF)):
                st, mv = (st1, mv1) if ln == "ln1" else (st23, mv23)
                for h in halves:
                    nc.vector.bn_stats(st[:, h, :], src[:, h, :]).then_inc(s[ln + "_raw"], 1)
                for h in halves:
                    wait_apart(dve, ln + "_raw", i * HALF + h + 1)
                    nc.vector.bn_aggr(mv[:, h, :], st[:, h, :]).then_inc(s[ln + "_stats"], 1)

            def normalise(i, ln, src, dst=xn):
                mv, rstd = (mv1, rstd1) if ln == "ln1" else (mv23, rstd23)
                for h in range(HALF):
                    dve.wait_ge(s[ln + "_rstd"], i * HALF + h + 1)
                    ts(dst[:, h, :], src[:, h, :], mv[:, h, 0:1], rstd[:, h:h + 1], ALU.subtract, ALU.mult).then_inc(s[ln + "_normed"], 1)

            def shift_mix(i):
                dve.wait_ge(s["h_ready"], (i + 1) * HALF)
                tt(xx[:], hT[:, :, 0:T], hT[:, :, 1:T + 1], ALU.subtract).then_inc(s["xx_ready"], 1)
                dve.wait_ge(s["xx_ready"], i + 1)
                for k in range(KT):
                    last = stt(out=xxx[:, k, :], in0=xx[:, k, :], scalar=maa[:, 0, k:k + 1], in1=hT[:, k, 1:T + 1], op0=ALU.mult, op1=ALU.add)
                last.then_inc(s["xxx_ready"], 1)

            def pair_of(n):
                return ps[:, 2 * n:2 * n + 2, :].rearrange("p a (k n) -> p (a k) n", n=T)

            def mixed(i, f):
                dve.wait_ge(s["mix_mm"], i * MIX + f + 1)
                if f == 2:
                    dve.wait_ge(s["zdec_mm"], i + 1)
                if f == 3:
                    dve.wait_ge(s["k_mm"], i + 1)
                if f == 4:
                    dve.wait_ge(s["v_mm"], i + 1)
                for k in range(KT):
                    last = stt(out=mixed_x[f % 2][:, k, :], in0=pair_of(f % 2)[:, k, :], scalar=maa[:, f + 1, k:k + 1],
                               in1=xx[:, k, :], op0=ALU.add, op1=ALU.mult)
                last.then_inc(s["mix_used"], 1)

            def time_mix(i, last_one):
                mixed(i, 2)
                if last_one is not None:
                    route_place(last_one)
                mixed(i, 3)
                dve.wait_ge(s["dd_mm"], i + 1)
                ts(e_tok[:], ps[:, 4:6, :], DECAY_CAP, None, ALU.min).then_inc(s["dd_capped"], 1)
                mixed(i, 4)
                decay_queries(i, 0)
                dve.wait_ge(s["g_tanh"], i + 1)
                stt(out=gT[:], in0=half_gate.rearrange("p h (k n) -> p (h k) n", n=T), scalar=1.0, in1=pair_of(3),
                    op0=ALU.add, op1=ALU.mult).then_inc(s["g_ready"], 1)

            def decay_queries(i, k):
                after(dve, "decays_ready", i * 8 + 2 * k + 2)
                dve.wait_ge(s["r_ready"], i + 1)
                q = lev[(k + 1) % 2]
                for slot in range(7):
                    half = 1 << (slot or 7)
                    upper = q[:, slot, :].rearrange("p (n two h) -> p n two h", two=2, h=half)[:, :, 1, :]
                    r = rT[:, k, :].rearrange("p (n two h) -> p n two h", two=2, h=half)[:, :, 1, :]
                    last = tt(upper, upper, r, ALU.mult)
                last.then_inc(s["r_decayed"], 1)

            def pick_near(i, h):
                wait_apart(dve, "far_copied", i * RH + h + 1)
                a = a_near[h % 2].rearrange("p t n -> p (t n)")
                for n in range(6):
                    if n % 2 == 0:
                        wait_apart(dve, "gram_near", i * (3 * RH) + 3 * h + n // 2 + 1)
                        if n:
                            wait_apart(dve, "near_picked", i * (3 * RH) + 3 * h + n // 2)
                    else:
                        wait_apart(dve, "level_picked", (i * RH + h) * 3 + n // 2 + 1)
                    nc.vector.copy_predicated(a, pick[:, n, :], ps[:, 2 + n // 2, (n % 2) * T:(n % 2 + 1) * T]
                                              ).then_inc(s["near_picked" if n % 2 else "level_picked"], 1)

            def group_stats(i, k):
                after(dve, "av_done", i * RH + 2 * k + 2)
                b = 6 + k % 2
                for n in range(4):
                    last = nc.vector.bn_stats(gst[:, k % 2, 6 * n:6 * n + 6], ps[:, b, n * HS:(n + 1) * HS])
                last.then_inc(s["gn_raw"], 1)
                wait_apart(dve, "gn_raw", i * KT + k + 1)
                for n in range(4):
                    last = nc.vector.bn_aggr(gmv[:, k % 2, 2 * n:2 * n + 2], gst[:, k % 2, 6 * n:6 * n + 6])
                last.then_inc(s["gn_stats"], 1)

            def group_norm(i, k):
                dve.wait_ge(s["gn_rstd"], i * KT + k + 1)
                b = 6 + k % 2
                for n in range(4):
                    t, p = divmod(n, 2)
                    last = ts(o_tok[:, t, k * P + p * HS:k * P + (p + 1) * HS], ps[:, b, n * HS:(n + 1) * HS],
                              gmv[:, k % 2, 2 * n:2 * n + 1], grstd[:, k % 2, n:n + 1], ALU.subtract, ALU.mult)
                last.then_inc(s["o_normed"], 1)

            def gate_and_add(i):
                dve.wait_ge(s["o_affine"], (i + 1) * KT)
                tt(oT[:], oT[:], gT[:], ALU.mult).then_inc(s["o_gated"], 1)
                window(i)
                after(dve, "x2_stored", i * 16)
                for h in range(HALF):
                    dve.wait_ge(s["wo_mm"], i * HALF + h + 1)
                    stt(out=x1[:, h, :], in0=ps[:, 2 + h, :], scalar=0.5, in1=x_in[:, h, :], op0=ALU.mult, op1=ALU.add).then_inc(s["x1_ready"], 1)
                    dve.wait_ge(s["x1_ready"], i * HALF + h + 1)
                    norm_stats(i, "ln2", x1, [h])

            def rotary_keys(i):
                dve.wait_ge(s["kr_mm"], i + 1)
                tt(kr_tmp, ps[:, 7, 0:T], ktab[:, 0, :], ALU.mult).then_inc(s["kr_cos"], 1)
                tt(krT, ps[:, 7, T:2 * T], ktab[:, 1, :], ALU.mult).then_inc(s["kr_sin"], 1)
                dve.wait_ge(s["kr_cos"], i + 1)
                dve.wait_ge(s["kr_sin"], i + 1)
                tt(krT, krT, kr_tmp, ALU.add).then_inc(s["kr_ready"], 1)

            def window(i):
                dve.wait_ge(s["seg_in"], (i + 1) * 16)
                nc.vector.tensor_copy(segf, segi.bitcast(I32)).then_inc(s["seg_float"], 1)
                dve.wait_ge(s["seg_float"], i + 1)
                for h in range(HALF):
                    n = i * HALF + h + 1
                    ts(late, keys, segf[:, h:h + 1], 0.0, ALU.subtract, ALU.is_gt).then_inc(s["late_set"], 1)
                    ts(early, keys, segf[:, h:h + 1], -float(LOOKBACK), ALU.subtract, ALU.is_lt).then_inc(s["early_set"], 1)
                    dve.wait_ge(s["late_set"], n)
                    dve.wait_ge(s["early_set"], n)
                    tt(late, late, early, ALU.add).then_inc(s["bad_set"], 1)
                    dve.wait_ge(s["bad_set"], n)
                    ts(bias[:, h, :], late, NEG, None, ALU.mult).then_inc(s["bias_ready"], 1)
                    dve.wait_ge(s["bias_ready"], n)

            UNITS = HALF * XH

            def head_query(i, u):
                dve.wait_ge(s["head_mm"], i * UNITS + u + 1)
                if u >= 2:
                    after(dve, "score_mm", i * UNITS + u - 1)
                tt(q_head[u % 2].rearrange("p a n -> p (a n)"), ps[:, u % 2, 0:2 * P], qtab[:, u // XH, :], ALU.mult).then_inc(s["head_ready"], 1)

            def row_max(i, u):
                dve.wait_ge(s["score_mm"], i * UNITS + u + 1)
                if u >= 4:
                    after(dve, "exp_done", i * UNITS + u - 3)
                nc.vector.tensor_reduce(negmax[:, u % 4:u % 4 + 1], ps[:, 2 + u % 2, 0:T], AX.X, ALU.max, negate=True).then_inc(s["max_ready"], 1)

            def divide(i, u):
                dve.wait_ge(s["exp_done"], i * UNITS + u + 1)
                nc.vector.reciprocal(prec[:, u % 4:u % 4 + 1], psumr[:, u % 4:u % 4 + 1]).then_inc(s["sum_inverted"], 1)
                dve.wait_ge(s["sum_inverted"], i * UNITS + u + 1)
                ts(prob[u % 3], prob[u % 3], prec[:, u % 4:u % 4 + 1], None, ALU.mult).then_inc(s["prob_ready"], 1)

            def add_cross(i, h):
                after(dve, "out_mm", i * UNITS + (h + 1) * XH)
                tt(x1[:, h, :], ps[:, 7, :], x1[:, h, :], ALU.add).then_inc(s["x2_ready"], 1)

            weights_of = weights[:].rearrange("p (n k) -> p n k", k=CHOICES)

            def route_norm(i):
                dve.wait_ge(s["x2_ready"], (i + 1) * HALF)
                norm_stats(i, "ln3", x1)
                normalise(i, "ln3", x1, x3)

            def route_choose(i):
                dve.wait_ge(s["logit_mm"], i + 1)
                nc.vector.tensor_copy(logit[:].rearrange("p h e -> p (h e)"), ps[:, 5, 0:HALF * E]).then_inc(s["route_link"], 1)
                wait_apart(dve, "route_link", i * 10 + 1)
                for h in range(HALF):
                    last = nc.vector.max(top[:, h, :], logit[:, h, :])
                last.then_inc(s["route_link"], 1)
                wait_apart(dve, "route_link", i * 10 + 2)
                for h in range(HALF):
                    last = nc.vector.max_index(topi[:, h, :], top[:, h, :], logit[:, h, :])
                last.then_inc(s["topi_ready"], 1)
                tt(odds[:, 0, :], top[:, :, 1], top[:, :, 0], ALU.subtract).then_inc(s["gap12"], 1)
                dve.wait_ge(s["topi_ready"], i + 1)
                nc.vector.tensor_copy(topf[:], topi[:]).then_inc(s["route_link"], 1)
                after(dve, "route_link", i * 10 + 3)
                for h in range(HALF):
                    for k in range(CHOICES):
                        last = ts(hot[:, h, k, :], iota_e[:], topf[:, h, k:k + 1], 1.0, ALU.is_equal, ALU.mult)
                last.then_inc(s["route_link"], 1)
                after(dve, "route_link", i * 10 + 4)
                tt(both[:], hot[:, :, 0, :], hot[:, :, 1, :], ALU.add).then_inc(s["both_ready"], 1)

            def route_place(i):
                dve.wait_ge(s["odds_ready"], i + 1)
                ts(odds[:, 2, :], odds[:, 1, :], 1.0, 2.0, ALU.add, ALU.mult).then_inc(s["route_link"], 1)
                after(dve, "route_link", i * 10 + 5)
                nc.vector.reciprocal(odds[:, 2, :], odds[:, 2, :]).then_inc(s["route_link"], 1)
                wait_apart(dve, "route_link", i * 10 + 6)
                tt(weights_of[:, bass.ds(i * HALF, HALF), 1], odds[:, 2, :], odds[:, 1, :], ALU.mult)
                nc.vector.tensor_copy(weights_of[:, bass.ds(i * HALF, HALF), 0], odds[:, 2, :]).then_inc(s["w_kept"], 1)
                dve.wait_ge(s["rank_mm"], i + 1)
                for h in range(HALF):
                    last = tt(place[:, h, :], ps[:, 5, (HALF + h) * E:(HALF + h + 1) * E], taken[:], ALU.add)
                last.then_inc(s["route_link"], 1)
                after(dve, "route_link", i * 10 + 7)
                tt(taken[:], ps[:, 5, 2 * HALF * E:2 * HALF * E + E], taken[:], ALU.add)
                tt(place[:, 1, :], ps[:, 5, 2 * HALF * E:2 * HALF * E + E], place[:, 1, :], ALU.add).then_inc(s["route_link"], 1)
                after(dve, "route_link", i * 10 + 8)
                tt(taken[:], ps[:, 5, 2 * HALF * E + E:3 * HALF * E], taken[:], ALU.add).then_inc(s["taken_moved"], 1)
                for h in range(HALF):
                    for k in range(CHOICES):
                        last = tt(picked[:, h, k, :], hot[:, h, k, :], place[:, h, :], ALU.mult)
                last.then_inc(s["route_link"], 1)
                after(dve, "route_link", i * 10 + 9)
                nc.vector.tensor_reduce(slotf[:], picked[:].rearrange("p h k e -> p (h k) e"), AX.X, ALU.add).then_inc(s["route_link"], 1)
                after(dve, "route_link", i * 10 + 10)
                after(dve, "scattered", i * (16 * HALF * CHOICES))
                nc.vector.tensor_copy(slot[:], slotf[:]).then_inc(s["slot_ready"], 1)
                nc.vector.tensor_copy(slots[:, bass.ds(i * (HALF * CHOICES), HALF * CHOICES)], slotf[:])
                nc.vector.tensor_copy(experts_of[:].rearrange("p (n k) -> p n k", k=CHOICES)[:, bass.ds(i * HALF, HALF), :],
                                      topf[:, :, 0:CHOICES]).then_inc(s["slots_kept"], 1)

            def step_table():
                links = [0]

                def link(ins):
                    links[0] += 1
                    ins.then_inc(s["table_link"], 1)
                    dve.wait_ge(s["table_link"], links[0])

                nc.vector.memset(zeros, 0.0).then_inc(s["zeros_set"], 1)
                shape = [P, E, E]
                tt(upto, iota_e[:].unsqueeze(1).to_broadcast(shape), iota_e[:].unsqueeze(2).to_broadcast(shape), ALU.is_le)
                link(tt(counts[:], taken[:], first_row[:], ALU.subtract))
                nc.vector.tensor_copy(count_int[:], counts[:]).then_inc(s["counted"], 1)
                link(ts(n_int[:], counts[:], float(P - 1), None, ALU.add))
                link(ts(n_int[:], n_int[:], 7, None, ALU.arith_shift_right))
                link(nc.vector.tensor_copy(n_tiles[:], n_int[:]))
                link(tt(spread, upto, n_tiles[:].unsqueeze(1).to_broadcast([P, E, E]), ALU.mult))
                link(nc.vector.tensor_reduce(ends[:, 0, :], spread, AX.X, ALU.add))
                shape = [P, STEPS + 2, E]
                link(tt(past, steps[:].unsqueeze(2).to_broadcast(shape), ends[:, 0, :].unsqueeze(1).to_broadcast(shape), ALU.is_ge))
                tt(past_tiles, past, n_tiles[:].unsqueeze(1).to_broadcast(shape), ALU.mult)
                link(nc.vector.tensor_reduce(step_e, past, AX.X, ALU.add))
                ts(step_base, step_e, float(REGION), None, ALU.mult)
                link(nc.vector.tensor_reduce(step_row, past_tiles, AX.X, ALU.add))
                link(tt(step_row, steps[:], step_row, ALU.subtract))
                link(stt(out=step_row, in0=step_row, scalar=float(P), in1=step_base, op0=ALU.mult, op1=ALU.add))
                ts(step_e, step_e, float(E - 1), None, ALU.min)
                link(ts(step_base, past[:, :, 0], -float(E), float(E - 1), ALU.mult, ALU.add))
                tt(step_tab[:, 0, :], step_e, step_base, ALU.add)
                ts(step_tab[:, 2, :], step_e, 1.0, None, ALU.add)
                ts(step_tab[:, 1, :], step_row, float(SPARE), None, ALU.min).then_inc(s["table_ready"], 1)
                link(tt(ends[:, 1, :], ends[:, 0, :], n_tiles[:], ALU.subtract))
                link(stt(out=ends[:, 1, :], in0=ends[:, 1, :], scalar=float(P), in1=first_row[:], op0=ALU.mult, op1=ALU.subtract))
                dve.wait_ge(s["slots_kept"], B)
                shape = [P, NT * CHOICES, E]
                link(tt(chosen, experts_of[:].unsqueeze(2).to_broadcast(shape), iota_e[:].unsqueeze(1).to_broadcast(shape), ALU.is_equal))
                link(tt(chosen, chosen, ends[:, 1, :].unsqueeze(1).to_broadcast(shape), ALU.mult))
                link(nc.vector.tensor_reduce(moved, chosen, AX.X, ALU.add))
                tt(rows[:], slots[:], moved, ALU.add).then_inc(s["rows_ready"], 1)

            dve.wait_ge(s["absorb_done"], 3 * XH)
            dve.wait_ge(s["router_in"], 16 * 6)
            dve.wait_ge(s["consts_in"], 32)
            nc.vector.tensor_copy(ident_bf[:], ident).then_inc(s["ident_bf_set"], 1)
            nc.vector.tensor_copy(pick.rearrange("p l n -> p (l n)"), pick_wide).then_inc(s["ident_bf_set"], 1)
            dve.wait_ge(s["ident_bf_set"], 2)
            dve.wait_ge(s["front_in"], 16 * 9)
            dve.wait_ge(s["ones_set"], 3)

            def first_norm(i):
                dve.wait_ge(s["x_in_loaded"], (i + 1) * 16)
                after(dve, "x1_transposed", i * HALF)
                norm_stats(i, "ln1", x_in)
                normalise(i, "ln1", x_in)

            def batch(i, last_one=None, next_one=None):
                if last_one is not None:
                    route_norm(last_one)
                shift_mix(i)
                mixed(i, 0)
                mixed(i, 1)
                if last_one is not None:
                    route_choose(last_one)
                time_mix(i, last_one)
                for h in range(RH):
                    k = h // 2
                    if h % 2 == 1 and k + 1 < KT:
                        decay_queries(i, k + 1)
                    pick_near(i, h)
                    if h >= 2 and h % 2 == 0:
                        group_stats(i, k - 1)
                    if h >= 3 and h % 2 == 1:
                        group_norm(i, k - 1)
                group_stats(i, KT - 1)
                group_norm(i, KT - 1)
                if last_one is None:
                    dve.wait_ge(s["cross_in"], 16 * 7)
                gate_and_add(i)
                normalise(i, "ln2", x1)
                rotary_keys(i)
                head_query(i, 0)
                for u in range(UNITS + 2):
                    if u < UNITS:
                        row_max(i, u)
                    if u + 1 < UNITS:
                        head_query(i, u + 1)
                    if u < UNITS:
                        divide(i, u)
                    if u == 4 and next_one is not None:
                        first_norm(next_one)
                    if u - 2 in (XH - 1, UNITS - 1):
                        add_cross(i, (u - 2) // XH)

            first_norm(0)
            batch(0, None, 1)
            with dve.Fori(1, B - 1) as i:
                batch(i, i - 1, i + 1)
            batch(B - 1, B - 2)
            route_norm(B - 1)
            route_choose(B - 1)
            route_place(B - 1)
            step_table()

            def inner(j):
                dve.wait_ge(s["m_tanhed"], j + 1)
                stt(out=m_silu, in0=m_tanh, scalar=1.0, in1=ps[:, 0, 0:I], op0=ALU.add, op1=ALU.mult).then_inc(s["m_silued"], 1)
                dve.wait_ge(s["up_mm"], j + 1)
                after(dve, "m_h_transposed", j)
                dve.wait_ge(s["m_silued"], j + 1)
                tt(m_h, m_silu, ps[:, 1, 0:I], ALU.mult).then_inc(s["m_h_ready"], 1)

            def finish(j, n):
                dve.wait_ge(s["down_mm"], j + 1)
                if not isinstance(j, int) or j >= 2:
                    after(dve, f"m_y_stored_{n}", (j - n) * 8)
                nc.vector.tensor_copy(m_y[n], ps[:, 5 + n, :]).then_inc(s["m_y_ready"], 1)

            inner(0)
            inner(1)
            finish(0, 0)
            with dve.Fori(1, STEPS // 2) as pair:
                for n in range(2):
                    j = pair * 2 + n
                    inner(j)
                    finish(j - 1, 1 - n)
            finish(STEPS - 1, 1)

            dve.wait_ge(s["res_in"], 16 * B)
            for n in range(NT):
                a = res[n // HALF][:, n % HALF, :]
                dve.wait_ge(y_in[n % Y_BUFFERS], 16 * CHOICES * (n // Y_BUFFERS + 1))
                for k in range(CHOICES):
                    w = weights[:, n * CHOICES + k:n * CHOICES + k + 1]
                    stt(out=a, in0=y_of[n % Y_BUFFERS][k], scalar=w, in1=a, op0=ALU.mult, op1=ALU.add).then_inc(s["summed" if k else "first_added"], 1)
                    if k == 0:
                        dve.wait_ge(s["first_added"], n + 1)

        @block.gpsimd
        def _(pool):
            def inverse_root(dst, var, eps, stats, n, done):
                wait_apart(pool, stats, n)
                nc.gpsimd.tensor_scalar(dst, var, eps, 1.0, ALU.add, ALU.mult).then_inc(s[done + "_sum"], 1)
                pool.wait_ge(s[done + "_sum"], n)
                nc.gpsimd.tensor_tensor(dst, dst, minus_half[:, 0:dst.shape[1]], ALU.pow).then_inc(s[done], 1)

            nc.gpsimd.memset(minus_half[:], -0.5).then_inc(s["ones_set"], 1)
            pool.wait_ge(s["absorb_done"], 3 * XH)
            pool.wait_ge(s["ones_set"], 1)
            nc.gpsimd.memset(z_dec[DDEC:DDEC + 1], 1.0).then_inc(s["ones_set"], 1)
            pool.wait_ge(s["ones_set"], 2)
            for p in range(2):
                nc.gpsimd.memset(a_near[p][:], 0.0)
            nc.gpsimd.memset(hT[:, :, 0:1], 0.0).then_inc(s["ones_set"], 1)
            pool.wait_ge(s["front_in"], 16 * 9)
            pool.wait_ge(s["ones_set"], 3)

            def layer_norm_roots(i, ln):
                mv, rstd = (mv1, rstd1) if ln == "ln1" else (mv23, rstd23)
                for h in range(HALF):
                    inverse_root(rstd[:, h:h + 1], mv[:, h, 1:2], LN_EPS, ln + "_stats", i * HALF + h + 1, ln + "_rstd")

            def mixed(i, f):
                pool.wait_ge(s["mix_used"], i * MIX + f + 1)
                nc.gpsimd.tensor_tensor(mixed_x[f % 2][:], mixed_x[f % 2][:], hT[:, :, 1:T + 1], ALU.add).then_inc(s["mixed_ready"], 1)

            def decay_keys(i, k):
                q = lev[(k + 1) % 2]
                pool.wait_ge(s["decays_ready"], i * 8 + 2 * k + 2)
                pool.wait_ge(s["k_ready"], i + 1)
                pool.wait_ge(s["r_ready"], i + 1)
                for slot in range(7):
                    half = 1 << (slot or 7)
                    lower = q[:, slot, :].rearrange("p (n two h) -> p n two h", two=2, h=half)[:, :, 0, :]
                    key = kT[:, k, :].rearrange("p (n two h) -> p n two h", two=2, h=half)[:, :, 0, :]
                    nc.gpsimd.tensor_tensor(lower, lower, key, ALU.mult)
                wait_apart(pool, "k_ready", i + 1)
                nc.gpsimd.tensor_scalar(ru[k % 2], rT[:, k, :], bonus[:, k:k + 1], 1.0, ALU.mult, ALU.mult).then_inc(s["k_decayed"], 1)

            def group_roots(i, k):
                v = gmv[:, k % 2, :].rearrange("p (n two) -> p n two", two=2)[:, :, 1]
                inverse_root(grstd[:, k % 2, :], v, GN_EPS, "gn_stats", i * KT + k + 1, "gn_rstd")

            def scatter(i):
                pool.wait_ge(s["ln3_normed"], (i + 1) * HALF)
                wait_apart(pool, "slot_ready", i + 1)
                for h in range(HALF):
                    for k in range(CHOICES):
                        at = bass.IndirectOffsetOnAxis(ap=slot[:, h * CHOICES + k:h * CHOICES + k + 1], axis=0)
                        pool.indirect_dma_start(xs, at, x3[:, h, :], None).then_inc(s["scattered"], 16)

            def batch(i, last_one=None, next_one=None):
                if last_one is not None:
                    layer_norm_roots(last_one, "ln3")
                for f in range(4):
                    mixed(i, f)
                if last_one is not None:
                    scatter(last_one)
                mixed(i, 4)
                decay_keys(i, 0)
                for k in range(KT):
                    if k + 1 < KT:
                        decay_keys(i, k + 1)
                    group_roots(i, k)
                layer_norm_roots(i, "ln2")
                if next_one is not None:
                    layer_norm_roots(next_one, "ln1")

            layer_norm_roots(0, "ln1")
            pool.wait_ge(s["h_ready"], HALF)
            batch(0, None, 1)
            with pool.Fori(1, B - 1) as i:
                batch(i, i - 1, i + 1)
            batch(B - 1, B - 2)
            layer_norm_roots(B - 1, "ln3")
            scatter(B - 1)
            pool.wait_ge(s["counted"], 1)
            pool.wait_ge(s["x2_stored"], 16 * B)
            pool.wait_ge(s["expert_in"], 16 * EARLY)
            pool.wait_ge(s["m_x_in_0"], 16)
            pool.wait_ge(s["m_x_in_1"], 16)
            pool.sem_inc(s["expert_ready"], EARLY)
            for e in range(EARLY, E):
                for part in range(2):
                    words = slice(part * E_WORDS // 2, (part + 1) * E_WORDS // 2)
                    pool.dma_start(block_of(e)[:, words], d["w_experts"][e][:, words]).then_inc(s["late_expert_in"], 16)
                    pool.wait_ge(s["late_expert_in"], 16 * ((e - EARLY) * 2 + part + 1))
                pool.sem_inc(s["expert_ready"], 1)
            pool.wait_ge(s["rows_ready"], 1)
            pool.wait_ge(s["padded"], 16 * (E + 1))
            for g in range(B):
                pool.dma_start(res[g][:], x2_dram[g]).then_inc(s["res_in"], 16)
            pool.wait_ge(s["down_mm"], STEPS)
            for n in range(2):
                pool.wait_ge(s[f"m_y_stored_{n}"], 16 * (STEPS // 2))
            for n in range(NT):
                if n >= Y_BUFFERS:
                    pool.wait_ge(s["summed"], n - Y_BUFFERS + 1)
                for k in range(CHOICES):
                    at = bass.IndirectOffsetOnAxis(ap=rows[:, n * CHOICES + k:n * CHOICES + k + 1], axis=0)
                    pool.indirect_dma_start(y_of[n % Y_BUFFERS][k], None, ys, at).then_inc(y_in[n % Y_BUFFERS], 16)


def _tiles(w, rows=P):
    k, n = w.shape
    return np.ascontiguousarray(w.reshape(k // rows, rows, n).transpose(1, 0, 2).reshape(rows, -1))


def _columns(v):
    v = v.reshape(-1, KT, P)
    return np.ascontiguousarray(v.transpose(2, 0, 1).reshape(P, -1))


def lay_out(n):
    a = {k[8:]: np.asarray(v) for k, v in n.items() if k.startswith("L0_attn_")}
    c = {k[9:]: np.asarray(v) for k, v in n.items() if k.startswith("L0_xattn_")}
    r = constants()
    r["c_iota"] = np.tile(np.arange(E, dtype=np.float32), (P, 1))
    r["c_first"] = np.tile(np.arange(E, dtype=np.float32) * REGION, (P, 1))
    r["c_steps"] = np.tile(np.arange(STEPS + 2, dtype=np.float32), (P, 1))
    r["x"] = np.ascontiguousarray(np.asarray(n["x"]).reshape(B, HALF, P, C).transpose(0, 2, 1, 3))
    ctx = np.asarray(n["ctx_2048"]).transpose(0, 2, 1).reshape(B, KT, P, T)
    r["ctxT"] = np.ascontiguousarray(ctx.transpose(0, 2, 1, 3).reshape(B, P, KT * T))
    r["seg"] = np.ascontiguousarray(np.asarray(n["itok_BxS_0_1023"]).reshape(B, HALF, P).transpose(0, 2, 1))
    r["w1"] = _tiles(a["time_maa_w1"])
    r["w2a"] = np.ascontiguousarray(a["time_maa_w2"][0:4].reshape(4 * DMIX, C))
    r["w2b"] = np.ascontiguousarray(a["time_maa_w2"][4])
    r["maa"] = _columns(np.concatenate([a["time_maa_" + f].reshape(1, C) for f in "xwkvrg"]))
    r["dw1"] = _tiles(a["time_decay_w1"])
    r["dw2"] = np.concatenate([a["time_decay_w2"], a["time_decay"].reshape(1, C)])
    r["bonus"] = _columns(a["time_faaaa"].reshape(1, C))
    r["gam"], r["bet"] = _columns(a["ln_gamma"]), _columns(a["ln_beta"])
    for f in "krvgo":
        r["w" + f] = _tiles(a["W_" + f].T)
    r["wkvc"], r["wdq"] = _tiles(c["W_kvc"]), _tiles(c["W_dq"])
    kr1, kr2 = np.split(c["W_kr"], 2, axis=1)
    r["wkr"] = np.concatenate([kr1, kr2, kr2, kr1, kr2, kr1, kr1, kr2], axis=1)
    r["wqr"] = _tiles(np.tile(c["W_qr"].reshape(QC, XH, 1, ROT), (1, 1, 2, 1)).reshape(QC, -1), QK)
    heads = lambda w: w.reshape(w.shape[0], XH, HD).transpose(2, 1, 0).reshape(HD, -1)
    r["uqT"], r["ukT"], r["uvT"] = (np.ascontiguousarray(heads(c[w])) for w in ("W_uq", "W_uk", "W_uv"))
    r["xo"] = np.ascontiguousarray(c["W_o"].reshape(XH, HD, C).transpose(1, 0, 2).reshape(HD, -1))
    r["router"] = _tiles(np.asarray(n["L0_ffn_router_w"]).T)
    w1 = np.asarray(n["L0_ffn_w1"])
    gate_up = w1.reshape(E, 2, I, KT, P).transpose(0, 4, 1, 3, 2).reshape(E, P, GU_WORDS)
    w2 = np.zeros((E, IT * P, C), np.float32)
    w2[:, :I] = np.asarray(n["L0_ffn_w2"]).transpose(0, 2, 1)
    down = w2.reshape(E, IT, P, C).transpose(0, 2, 1, 3).reshape(E, P, IT * C)
    r["w_experts"] = np.ascontiguousarray(np.concatenate([gate_up, down], 2))
    return r


def kernel(**inputs):
    import concourse.bacc as bacc
    from concourse.bass_utils import run_bass_kernel_spmd

    arrays = lay_out(inputs)
    nc = bacc.Bacc("TRN2", target_bir_lowering=False, num_devices=1)
    dram = {k: nc.dram_tensor("in_" + k, v.shape, mybir.dt.from_np(v.dtype), kind="ExternalInput").ap()
            for k, v in arrays.items()}
    out = nc.dram_tensor("out_x", (B, T, C), F32, kind="ExternalOutput").ap()
    x2 = nc.dram_tensor("x2_scratch", (B, P, HALF, C), F32, kind="Internal").ap()
    xs = nc.dram_tensor("routed_tokens", (SPARE + P, C), F32, kind="Internal").ap()
    ys = nc.dram_tensor("routed_results", (STEPS * P, C), F32, kind="Internal").ap()
    program(nc, dram, out, x2, xs, ys)
    r = run_bass_kernel_spmd(nc, [{"in_" + k: v for k, v in arrays.items()}], core_ids=[0])
    return r.results[0]["out_x"]
```
